# Optimizing a Trainium2 kernel written in Bass

```python
import numpy as np
import jax
import jax.numpy as jnp

def _softmax(x, axis=-1):
    return jax.nn.softmax(x, axis=axis)

def _gelu(x):
    return jax.nn.gelu(x, approximate=True)

def _silu(x):
    return jax.nn.silu(x)

def _sigmoid(x):
    return jax.nn.sigmoid(x)

def _layernorm(x, axis=-1, eps=1e-05):
    m = jnp.mean(x, axis=axis, keepdims=True)
    v = jnp.var(x, axis=axis, keepdims=True)
    return (x - m) / jnp.sqrt(v + eps)

def _scatter_add(tgt, idx, src, axis=0):
    return tgt.at[idx].add(src)

def _segment_sum(src, seg, n):
    return jax.ops.segment_sum(src, seg, n)
kernel_name = 'mk_xattn_seq_d2_seqx_r4_4d7997'

def setup_inputs(seed: int=0):
    np.random.seed(seed)
    _w = jnp.asarray

    def _rec_inputs():
        import jax
        import jax.numpy as jnp
        _rk = jax.random.key(seed)
        x = 7.22e-05 + 1 * jax.random.normal(jax.random.fold_in(_rk, 1), (64, 128, 256), jnp.float32)
        _lenS = 128 - jax.random.randint(jax.random.fold_in(_rk, 7), (64,), 0, max(1, 128 // 4) + 1, jnp.int32)
        _lenS2 = 128 - jax.random.randint(jax.random.fold_in(_rk, 8), (64,), 0, max(1, 128 // 4) + 1, jnp.int32)
        _ctx_1024P = jax.random.normal(jax.random.fold_in(_rk, 11), (64, 16, 256), jnp.float32)
        _ctx_1024c = jax.random.dirichlet(jax.random.fold_in(_rk, 511), 0.3 * jnp.ones((16,), jnp.float32), (64, 128))
        _ctx_1024t = jnp.einsum('bsk,bkd->bsd', _ctx_1024c, _ctx_1024P)
        _ctx_1024t = _ctx_1024t * jax.lax.rsqrt(jnp.mean(jnp.square(_ctx_1024t)) + 1e-12) * 0.953939
        ctx_1024 = 4.13588e-05 + 0.999923 * (_ctx_1024t + 0.3 * jax.random.normal(jax.random.fold_in(_rk, 611), (64, 128, 256), jnp.float32))
        return (x, ctx_1024)
    x, ctx_1024 = _rec_inputs()

    def _L0_xattn_setup():
        import jax, jax.numpy as jnp
        import numpy as np
        D, H, HS, NTOK, EPS = (256, 16, 64, 512, 1e-05)

        def _ln(x, g, b):
            m = jnp.mean(x, axis=-1, keepdims=True)
            v = jnp.mean((x - m) ** 2, axis=-1, keepdims=True)
            return (x - m) * jax.lax.rsqrt(v + EPS) * g + b
        key = jax.random.key(seed)
        ks = jax.random.split(key, 16)
        B, T = (4, 512)
        s = lambda k, shape, sc=0.02: jax.random.normal(k, shape, jnp.float32) * sc
        return {'q': jax.random.normal(ks[0], (B, T, D), jnp.float32), 'k': jax.random.normal(ks[1], (B, T, D), jnp.float32), 'v': jax.random.normal(ks[2], (B, T, D), jnp.float32), 'ln_q_g': jnp.ones((D,), jnp.float32), 'ln_q_b': jnp.zeros((D,), jnp.float32), 'ln_k_g': jnp.ones((D,), jnp.float32), 'ln_k_b': jnp.zeros((D,), jnp.float32), 'ln_v_g': jnp.ones((D,), jnp.float32), 'ln_v_b': jnp.zeros((D,), jnp.float32), 'Wq': s(ks[3], (H, HS, D)), 'Wk': s(ks[4], (H, HS, D)), 'Wv': s(ks[5], (H, HS, D)), 'fc_w': s(ks[6], (D, H * HS)), 'fc_b': jnp.zeros((D,), jnp.float32), 'rel_bias': s(ks[7], (2 * NTOK - 1,)), 'ln2_g': jnp.ones((D,), jnp.float32), 'ln2_b': jnp.zeros((D,), jnp.float32), 'W1': s(ks[8], (4 * D, D)), 'b1': jnp.zeros((4 * D,), jnp.float32), 'W2': s(ks[9], (D, 4 * D)), 'b2': jnp.zeros((D,), jnp.float32)}
    _L0_xattn_all = _L0_xattn_setup()
    _L0_xattn_in = {k: v for k, v in _L0_xattn_all.items() if k in ('ln_q_g', 'ln_q_b', 'ln_k_g', 'ln_k_b', 'ln_v_g', 'ln_v_b', 'Wq', 'Wk', 'Wv', 'fc_w', 'fc_b', 'rel_bias', 'ln2_g', 'ln2_b', 'W1', 'b1', 'W2', 'b2')}
    del _L0_xattn_all

    def _L1_xattn_setup():
        import jax, jax.numpy as jnp
        import numpy as np
        D_MODEL = 256
        N_HEADS = 16
        N_KV_HEADS = 1
        HEAD_DIM = D_MODEL // N_HEADS
        WINDOW = 128
        EPS = 1e-06
        NEG = -1000000000.0

        def _window_mask(S):
            i = jnp.arange(S)[:, None]
            j = jnp.arange(S)[None, :]
            half = WINDOW // 2
            return (j >= i - half) & (j < i + half + 1)
        key = jax.random.key(seed)
        ks = jax.random.split(key, 16)
        B, S, D = (2, 512, D_MODEL)
        kv_out = HEAD_DIM * N_KV_HEADS
        s = 0.02
        return {'query': jax.random.normal(ks[0], (B, S, D), jnp.float32), 'key': jax.random.normal(ks[1], (B, S, D), jnp.float32), 'value': jax.random.normal(ks[2], (B, S, D), jnp.float32), 'Wq': jax.random.normal(ks[3], (D, D), jnp.float32) * s, 'bq': jnp.zeros((D,), jnp.float32), 'Wk': jax.random.normal(ks[4], (D, kv_out), jnp.float32) * s, 'bk': jnp.zeros((kv_out,), jnp.float32), 'Wv': jax.random.normal(ks[5], (D, kv_out), jnp.float32) * s, 'bv': jnp.zeros((kv_out,), jnp.float32), 'Wo': jax.random.normal(ks[6], (D, D), jnp.float32) * s, 'bo': jnp.zeros((D,), jnp.float32), 'Wg': jax.random.normal(ks[7], (2 * D, D), jnp.float32) * s, 'bg': jnp.zeros((D,), jnp.float32), 'rms_w': jnp.ones((D,), jnp.float32)}
    _L1_xattn_all = _L1_xattn_setup()
    _L1_xattn_in = {k: v for k, v in _L1_xattn_all.items() if k in ('Wq', 'bq', 'Wk', 'bk', 'Wv', 'bv', 'Wo', 'bo', 'Wg', 'bg', 'rms_w')}
    del _L1_xattn_all
    return {'x': x, 'ctx_1024': ctx_1024, 'L0_xattn_ln_q_g': _L0_xattn_in['ln_q_g'], 'L0_xattn_ln_q_b': _L0_xattn_in['ln_q_b'], 'L0_xattn_ln_k_g': _L0_xattn_in['ln_k_g'], 'L0_xattn_ln_k_b': _L0_xattn_in['ln_k_b'], 'L0_xattn_ln_v_g': _L0_xattn_in['ln_v_g'], 'L0_xattn_ln_v_b': _L0_xattn_in['ln_v_b'], 'L0_xattn_Wq': _L0_xattn_in['Wq'], 'L0_xattn_Wk': _L0_xattn_in['Wk'], 'L0_xattn_Wv': _L0_xattn_in['Wv'], 'L0_xattn_fc_w': _L0_xattn_in['fc_w'], 'L0_xattn_fc_b': _L0_xattn_in['fc_b'], 'L0_xattn_rel_bias': _L0_xattn_in['rel_bias'], 'L0_xattn_ln2_g': _L0_xattn_in['ln2_g'], 'L0_xattn_ln2_b': _L0_xattn_in['ln2_b'], 'L0_xattn_W1': _L0_xattn_in['W1'], 'L0_xattn_b1': _L0_xattn_in['b1'], 'L0_xattn_W2': _L0_xattn_in['W2'], 'L0_xattn_b2': _L0_xattn_in['b2'], 'L1_xattn_Wq': _L1_xattn_in['Wq'], 'L1_xattn_bq': _L1_xattn_in['bq'], 'L1_xattn_Wk': _L1_xattn_in['Wk'], 'L1_xattn_bk': _L1_xattn_in['bk'], 'L1_xattn_Wv': _L1_xattn_in['Wv'], 'L1_xattn_bv': _L1_xattn_in['bv'], 'L1_xattn_Wo': _L1_xattn_in['Wo'], 'L1_xattn_bo': _L1_xattn_in['bo'], 'L1_xattn_Wg': _L1_xattn_in['Wg'], 'L1_xattn_bg': _L1_xattn_in['bg'], 'L1_xattn_rms_w': _L1_xattn_in['rms_w']}

def reference(x, ctx_1024, L0_xattn_ln_q_g, L0_xattn_ln_q_b, L0_xattn_ln_k_g, L0_xattn_ln_k_b, L0_xattn_ln_v_g, L0_xattn_ln_v_b, L0_xattn_Wq, L0_xattn_Wk, L0_xattn_Wv, L0_xattn_fc_w, L0_xattn_fc_b, L0_xattn_rel_bias, L0_xattn_ln2_g, L0_xattn_ln2_b, L0_xattn_W1, L0_xattn_b1, L0_xattn_W2, L0_xattn_b2, L1_xattn_Wq, L1_xattn_bq, L1_xattn_Wk, L1_xattn_bk, L1_xattn_Wv, L1_xattn_bv, L1_xattn_Wo, L1_xattn_bo, L1_xattn_Wg, L1_xattn_bg, L1_xattn_rms_w):
    import jax
    import jax.numpy as jnp

    def _L0_xattn_ref(q, k, v, ln_q_g, ln_q_b, ln_k_g, ln_k_b, ln_v_g, ln_v_b, Wq, Wk, Wv, fc_w, fc_b, rel_bias, ln2_g, ln2_b, W1, b1, W2, b2):
        import jax, jax.numpy as jnp
        import numpy as np
        D, H, HS, NTOK, EPS = (256, 16, 64, 512, 1e-05)

        def _ln(x, g, b):
            m = jnp.mean(x, axis=-1, keepdims=True)
            v = jnp.mean((x - m) ** 2, axis=-1, keepdims=True)
            return (x - m) * jax.lax.rsqrt(v + EPS) * g + b
        B, T, _ = q.shape
        qn = _ln(q, ln_q_g, ln_q_b)
        kn = _ln(k, ln_k_g, ln_k_b)
        vn = _ln(v, ln_v_g, ln_v_b)
        qh = jnp.einsum('btd,hed->bhte', qn, Wq)
        kh = jnp.einsum('btd,hed->bhte', kn, Wk)
        vh = jnp.einsum('btd,hed->bhte', vn, Wv)
        attn = jnp.einsum('bhte,bhse->bhts', qh, kh)
        idx = jnp.arange(T)[:, None] - jnp.arange(T)[None, :] + NTOK - 1
        attn = attn + rel_bias[idx]
        scale = jnp.float32(HS) ** 0.5
        p = jax.nn.softmax(attn / scale, axis=-1)
        out = jnp.einsum('bhts,bhse->bhte', p, vh)
        out = out.transpose(0, 2, 1, 3).reshape(B, T, H * HS)
        attn_out = out @ fc_w.T + fc_b
        x = q + attn_out
        h = _ln(x, ln2_g, ln2_b)
        ff = jax.nn.gelu(h @ W1.T + b1, approximate=False) @ W2.T + b2
        return x + ff

    def _L1_xattn_ref(query, key, value, Wq, bq, Wk, bk, Wv, bv, Wo, bo, Wg, bg, rms_w):
        import jax, jax.numpy as jnp
        import numpy as np
        D_MODEL = 256
        N_HEADS = 16
        N_KV_HEADS = 1
        HEAD_DIM = D_MODEL // N_HEADS
        WINDOW = 128
        EPS = 1e-06
        NEG = -1000000000.0

        def _window_mask(S):
            i = jnp.arange(S)[:, None]
            j = jnp.arange(S)[None, :]
            half = WINDOW // 2
            return (j >= i - half) & (j < i + half + 1)
        B, S, D = query.shape
        q = (query @ Wq + bq).reshape(B, S, N_HEADS, HEAD_DIM).transpose(0, 2, 1, 3)
        k = (key @ Wk + bk).reshape(B, S, N_KV_HEADS, HEAD_DIM).transpose(0, 2, 1, 3)
        v = (value @ Wv + bv).reshape(B, S, N_KV_HEADS, HEAD_DIM).transpose(0, 2, 1, 3)
        scale = 1.0 / jnp.sqrt(jnp.float32(HEAD_DIM))
        scores = jnp.matmul(q, jnp.swapaxes(k, -1, -2)) * scale
        keep = _window_mask(S)
        scores = jnp.where(keep[None, None], scores, NEG)
        probs = jax.nn.softmax(scores, axis=-1)
        attn = jnp.matmul(probs, v)
        attn = attn.transpose(0, 2, 1, 3).reshape(B, S, D)
        attn = attn @ Wo + bo
        gate = jax.nn.silu(jnp.concatenate([attn, query], axis=-1) @ Wg + bg)
        out = attn * gate + query * (1.0 - gate)
        x_hat = out * jax.lax.rsqrt(jnp.mean(out * out, axis=-1, keepdims=True) + EPS) * rms_w
        return x_hat - jnp.mean(x_hat, axis=1, keepdims=True)
    x = _L0_xattn_ref(x, ctx_1024, ctx_1024, L0_xattn_ln_q_g, L0_xattn_ln_q_b, L0_xattn_ln_k_g, L0_xattn_ln_k_b, L0_xattn_ln_v_g, L0_xattn_ln_v_b, L0_xattn_Wq, L0_xattn_Wk, L0_xattn_Wv, L0_xattn_fc_w, L0_xattn_fc_b, L0_xattn_rel_bias, L0_xattn_ln2_g, L0_xattn_ln2_b, L0_xattn_W1, L0_xattn_b1, L0_xattn_W2, L0_xattn_b2)
    x = _L1_xattn_ref(x, ctx_1024, ctx_1024, L1_xattn_Wq, L1_xattn_bq, L1_xattn_Wk, L1_xattn_bk, L1_xattn_Wv, L1_xattn_bv, L1_xattn_Wo, L1_xattn_bo, L1_xattn_Wg, L1_xattn_bg, L1_xattn_rms_w)
    return x

_drawn_inputs = setup_inputs


def setup_inputs(seed=0):
    import zlib

    import numpy as np

    out = dict(_drawn_inputs(seed))
    spreads = {'L0_xattn_ln_q_g': (1.0, 0.6),
     'L0_xattn_ln_q_b': (0.0, 0.8),
     'L0_xattn_ln_k_g': (1.0, 0.6),
     'L0_xattn_ln_k_b': (0.0, 2.0),
     'L0_xattn_ln_v_g': (1.0, 0.6),
     'L0_xattn_ln_v_b': (0.0, 0.8),
     'L0_xattn_fc_b': (0.0, 0.271),
     'L0_xattn_ln2_g': (1.0, 0.6),
     'L0_xattn_ln2_b': (0.0, 0.8),
     'L0_xattn_b1': (0.0, 0.475),
     'L0_xattn_b2': (0.0, 0.319),
     'L1_xattn_bq': (0.0, 0.8),
     'L1_xattn_bk': (0.0, 2.0),
     'L1_xattn_bv': (0.0, 0.8),
     'L1_xattn_bo': (0.0, 0.324),
     'L1_xattn_bg': (0.0, 0.1),
     'L1_xattn_rms_w': (1.0, 0.2)}
    factors = {'L0_xattn_Wq': 8.0,
     'L0_xattn_Wk': 8.0,
     'L0_xattn_rel_bias': 200.0,
     'L1_xattn_Wq': 8.0,
     'L1_xattn_Wk': 8.0,
     'L1_xattn_Wv': 4.274,
     'L1_xattn_Wo': 3.571}
    for name, (base, spread) in spreads.items():
        noise = np.random.default_rng([zlib.crc32(name.encode()), seed]).standard_normal(out[name].shape)
        drawn = base * np.exp(spread * noise) if base else spread * noise
        out[name] = jnp.asarray(drawn.astype(out[name].dtype))
    for name, factor in factors.items():
        out[name] = (out[name] * factor).astype(out[name].dtype)
    return out
```

```python
from contextlib import ExitStack

import numpy as np

import concourse.bass as bass
from concourse import mybir

F32 = mybir.dt.float32
F32R = mybir.dt.float32r
ALU = mybir.AluOpType
ACT = mybir.ActivationFunctionType

P = 128
HI, LO = 0, 1
BANKS, BANK = 8, 512


class Steps:

    ENGINES = ("sync", "tensor", "vector", "scalar", "gpsimd")

    def __init__(self, nc, ctx):
        self.nc, self.ctx = nc, ctx
        self.queue = {e: [] for e in self.ENGINES}
        self.sem, self.count, self.engine_of = {}, {}, {}
        self.passed = {e: {} for e in self.ENGINES}

    def step(self, engine, name, work, after=(), by=1):
        if name not in self.sem:
            self.sem[name] = self.ctx.enter_context(self.nc.semaphore(name))
            self.count[name], self.engine_of[name] = 0, engine
        assert self.engine_of[name] == engine
        waits = []
        for token in after:
            if token is None:
                continue
            other, value = token
            if self.passed[engine].get(other, 0) < value:
                self.passed[engine][other] = value
                waits.append((self.sem[other], value))
        self.count[name] += by
        self.queue[engine].append((waits, work, self.sem[name], by))
        return name, self.count[name]

    def load(self, name, work, after=()):
        return self.step("sync", name, work, after, by=16)

    def replay(self, engine, eng):
        for waits, work, sem, by in self.queue[engine]:
            for other, value in waits:
                eng.wait_ge(other, value)
            work(eng).then_inc(sem, by)


class Banks:

    def __init__(self, tiles):
        self.tiles, self.free = tiles, [(i, None) for i in range(len(tiles))]

    def take(self):
        index, token = self.free.pop(0)
        return index, self.tiles[index], token

    def give(self, index, token):
        self.free.append((index, token))


def two_block_xattn(nc, t):
    NBATCH, SEQ, D = t["x"].shape
    GROUP = 2
    NG = NBATCH // GROUP
    KD = D // P
    TOK = GROUP * SEQ
    F = t["wq_t"].shape[1]
    H0 = 16
    HS = F // H0
    NC_F = F // P
    QUAD = BANK // SEQ
    NQ = H0 // QUAD
    QC = QUAD * HS // P
    QW = QUAD * HS
    H1 = 16
    HD = D // H1
    HPC = P // HD
    NU1 = H1 // QUAD
    WINDOW_HALF = 64
    EPS0, EPS1 = 1e-5, 1e-6
    SCALE0, SCALE1 = float(HS) ** -0.5, float(HD) ** -0.5
    MASKED = -1e30
    LOWEST = -3.0e38
    assert SEQ == P and D == 256

    with ExitStack() as ctx:
        S = Steps(nc, ctx)
        step, load = S.step, S.load

        def sb(name, shape, dt=F32):
            return ctx.enter_context(nc.sbuf_tensor(name, shape, dt))

        banks = Banks([ctx.enter_context(nc.psum_tensor(f"bank{i}", [P, BANK], F32)) for i in range(BANKS)])

        wq = sb("wq", [P, 2, KD, F], F32R)
        wk = sb("wk", [P, 2, KD, F], F32R)
        wv = sb("wv", [P, 2, KD, F], F32R)
        wfc = sb("wfc", [P, 2, NC_F, D], F32R)
        w1 = sb("w1", [P, 2, KD, F], F32R)
        w2 = sb("w2", [P, 2, NC_F, D], F32R)
        wq1 = sb("wq1", [P, KD, D])
        wkv1 = sb("wkv1", [P, 2, KD, HD])
        wk1 = sb("wk1", [P, KD, P])
        wog = sb("wog", [P, KD, 2 * D])
        wgx = sb("wgx", [P, KD, D])
        gains = sb("gains", [P, 3 + 1, KD])
        shifts = sb("shifts", [P, 3 + 1, KD])
        ident = sb("ident", [P, P])
        center = sb("center", [P, P])
        relb = sb("relb", [P, SEQ])
        winb = sb("winb", [P, SEQ])
        block_of = sb("block_of", [P, HPC])
        ones = sb("ones", [P, P])
        half_exp = sb("half_exp", [P, 4])
        bq = sb("bq", [P, NC_F])
        bk = sb("bk", [P, NC_F])
        bv = sb("bv", [P, NC_F])
        b1 = sb("b1", [P, NC_F])
        bq1 = sb("bq1", [P, KD])
        bk1 = sb("bk1", [P, 1])
        bo_col = sb("bo_col", [P, KD])
        fcb = sb("fcb", [P, D])
        b2 = sb("b2", [P, D])
        bog = sb("bog", [P, 2 * D])
        bv1 = sb("bv1", [P, HD])
        rmsw = sb("rmsw", [P, D])
        X = sb("X", [P, 2, GROUP, D])
        C = sb("C", [P, 2, GROUP, D])
        NT = 4
        normed = sb("normed", [P, NT, D])
        stats = sb("stats", [P, 4, 6])
        moments = sb("moments", [P, 4, 2])
        rstd = sb("rstd", [P, 4])
        stats2 = sb("stats2", [P, GROUP, 6])
        moments2 = sb("moments2", [P, GROUP, 2])
        rstd2 = sb("rstd2", [P, GROUP])
        xT = sb("xT", [P, 2, KD, TOK], F32R)
        cT = sb("cT", [P, 2, KD, TOK], F32R)
        hT = sb("hT", [P, 2, KD, TOK], F32R)
        rawcT = sb("rawcT", [P, KD, TOK])
        qT = sb("qT", [P, 2, QC, TOK])
        kT = sb("kT", [P, 2, QC, TOK])
        V = sb("V", [P, 2, GROUP, QW])
        OT = sb("OT", [P, 2, GROUP, QC, SEQ], F32R)
        NS = 4
        soft = sb("soft", [P, NS, QUAD, SEQ])
        softT = sb("softT", [P, NS, QUAD, SEQ])
        row_max = sb("row_max", [P, NS, QUAD])
        neg_max = sb("neg_max", [P, NS, QUAD])
        row_sum = sb("row_sum", [P, NS, QUAD])
        inv_sum = sb("inv_sum", [P, NS, QUAD])
        x1 = sb("x1", [P, GROUP, D])
        HH = NC_F // 2
        hid = sb("hid", [P, HH, TOK])
        hidS = sb("hidS", [P, 2, HH, TOK], F32R)
        x2T = sb("x2T", [P, KD, TOK])
        q1T = sb("q1T", [P, KD, TOK])
        NK1 = 3
        k1T = sb("k1T", [P, NK1, TOK])
        v1 = sb("v1", [P, NK1, GROUP, HD])
        kblock = sb("kblock", [P, HPC, SEQ])
        VSTEP = P + HD
        vpad = sb("vpad", [P, HPC * VSTEP])
        o1T = sb("o1T", [P, KD, SEQ])
        ag = sb("ag", [P, 2 * D])
        gate = sb("gate", [P, D])
        mixed = sb("mixed", [P, D])
        sumsq = sb("sumsq", [P, 1])
        rrms = sb("rrms", [P, 1])
        Y = sb("Y", [P, D])

        def f32(ap):
            return ap.bitcast(F32)

        def mm3(pe, out, stat, mov, first, last, **kw):
            pe.matmul(out, stat(LO), mov(HI), start=first, stop=False, **kw)
            pe.matmul(out, stat(HI), mov(LO), start=False, stop=False, **kw)
            return pe.matmul(out, stat(HI), mov(HI), start=False, stop=last, **kw)

        def bcast(ap):
            return ap.partition_broadcast(P)

        small = []
        for i, n in enumerate(("ln_q", "ln_k", "ln_v", "ln2")):
            small.append((gains[:, i, :], t[n + "_g"]))
            small.append((shifts[:, i, :], t[n + "_b"]))
        small += [(relb[:], t["rel"]), (fcb[:], bcast(t["fc_b"])), (b2[:], bcast(t["b2"])),
                  (b1[:], t["b1"]), (bq1[:], t["bq1"]), (bo_col[:], t["bo_col"]),
                  (bog[:, 0:D], bcast(t["bo"])), (bog[:, D:2 * D], bcast(t["bg"])),
                  (bv1[:], bcast(t["bv1"])), (rmsw[:], bcast(t["rms_w"])),
                  (wq1[:], t["wq1"].rearrange("(k p) n -> p k n", p=P)),
                  (wkv1[:, 0, :, :], t["wk1"].rearrange("(k p) n -> p k n", p=P)),
                  (wkv1[:, 1, :, :], t["wv1"].rearrange("(k p) n -> p k n", p=P)),
                  (wog[:, :, 0:D], t["wo"].rearrange("(k p) n -> p k n", p=P)),
                  (wgx[:], t["wg"][D:2 * D, :].rearrange("(k p) n -> p k n", p=P))]
        small += [(bk1[HD * j:HD * (j + 1), :], t["bk1"].rearrange("(p o) -> p o", o=1)) for j in range(HPC)]

        def load_small(sp):
            for dst, src in small[:-1]:
                sp.dma_start(dst, src).then_inc(S.sem["consts"], 16)
            return sp.dma_start(*small[-1])
        S.sem["consts"] = ctx.enter_context(nc.semaphore("consts"))
        S.count["consts"], S.engine_of["consts"] = 16 * (len(small) - 1), "sync"
        consts = load("consts", load_small)

        def pool_consts(pool):
            pool.memset(half_exp[:], -0.5)
            pool.memset(ones[:], 1.0)
            pool.memset(ident[:], 0.0)
            pool.memset(center[:], -1.0 / SEQ)
            pool.memset(winb[:], 0.0)
            pool.memset(block_of[:], 1.0)
            return pool.memset(vpad[:], 0.0)
        filled = step("gpsimd", "filled", pool_consts)

        def pool_select(pool):
            pool.affine_select(out=ident[:], in_=ident[:], compare_op=ALU.not_equal, fill=1.0, base=0,
                               pattern=[[-1, P]], channel_multiplier=1)
            pool.affine_select(out=center[:], in_=center[:], compare_op=ALU.not_equal, fill=1.0 - 1.0 / SEQ,
                               base=0, pattern=[[-1, P]], channel_multiplier=1)
            pool.affine_select(out=winb[:], in_=winb[:], compare_op=ALU.is_ge, fill=MASKED,
                               base=WINDOW_HALF, pattern=[[1, SEQ]], channel_multiplier=-1)
            return pool.affine_select(out=block_of[:], in_=block_of[:], compare_op=ALU.is_ge, fill=0.0, base=0,
                                      pattern=[[-HD, HPC]], channel_multiplier=1)
        selected = step("gpsimd", "selected", pool_select, [filled])

        def pool_select2(pool):
            pool.affine_select(out=winb[:], in_=winb[:], compare_op=ALU.is_ge, fill=MASKED,
                               base=WINDOW_HALF, pattern=[[-1, SEQ]], channel_multiplier=1)
            return pool.affine_select(out=block_of[:], in_=block_of[:], compare_op=ALU.is_ge, fill=0.0,
                                      base=HD - 1, pattern=[[HD, HPC]], channel_multiplier=-1)
        masks = step("gpsimd", "selected", pool_select2, [selected])

        stage = [hid[:].rearrange("p a b -> p (a b)"), kblock[:].rearrange("p a b -> p (a b)")]
        stage_free = [None, None]
        HALF = KD * F // 2
        bias_done = {}

        def prepare(n, name, src, dst, gain, bias_cols):
            slot = prepare.count % 2
            prepare.count += 1
            buf = stage[slot]
            raw = load(f"raw{slot}", lambda sp: sp.dma_start(
                buf if len(src.shape) == 2 else buf.rearrange("p (c n) -> p c n", c=src.shape[1]), src),
                [stage_free[slot]])
            used = None
            if bias_cols is not None:
                shift, out_bank, taken = bias_cols

                def bias_mm(pe):
                    for c in range(NC_F):
                        last = pe.matmul(out_bank[:, c:c + 1], buf[:, c * P:(c + 1) * P], shifts[:, shift, n:n + 1],
                                         start=(n == 0 and c == 0), stop=(n == KD - 1), skip_group_check=True)
                    return last
                used = step("tensor", "bias_mm", bias_mm, [raw, consts, taken])
                bias_done[name] = used
            ready = raw
            if gain is not None:
                ready = step("vector", "scaled", lambda v: v.tensor_scalar(
                    buf, buf, gains[:, gain, n:n + 1], None, ALU.mult), [raw, consts, used])
            hi = step("scalar", "w_hi", lambda a: a.copy(dst(HI), buf), [ready])
            lo = step("vector", "w_lo", lambda v: v.tensor_tensor(dst(LO), buf, f32(dst(HI)), ALU.subtract),
                      [ready, hi])
            stage_free[slot] = lo
            return lo
        prepare.count = 0

        def half_k(w):
            return lambda n: (lambda part: w[:, part, n, :])

        def half_c(w):
            half = NC_F // 2
            return lambda n: (lambda part: w[:, part, n * half:(n + 1) * half, :].rearrange("p c n -> p (c n)"))

        for name, w, idx, src, bias in (("q", wq, 0, "wq_t", bq), ("k", wk, 1, "wk_t", bk), ("v", wv, 2, "wv_t", bv),
                                        ("1", w1, 3, "w1_t", b1)):
            index, bank, taken = banks.take()
            for n in range(KD):
                prepare(n, name, t[src][n * P:(n + 1) * P, :], half_k(w)(n), idx, (idx, bank, taken))
            if name == "1":
                done = step("vector", "bias", lambda v, bank=bank: v.tensor_tensor(
                    b1[:], bank[:, 0:NC_F], b1[:], ALU.add), [bias_done[name], consts])
            else:
                done = step("vector", "bias", lambda v, bank=bank, bias=bias: v.tensor_copy(
                    bias[:], bank[:, 0:NC_F]), [bias_done[name]])
            banks.give(index, done)
            bias_done[name] = done
        for w, src in ((wfc, "fc_t"), (w2, "w2_t")):
            for n in range(2):
                rows = F // 2
                weights = prepare(n, src, t[src][n * rows:(n + 1) * rows, :].rearrange("(c p) n -> p c n", p=P),
                                  half_c(w)(n), None, None)

        bcol = x1[:, :, 0:P]
        index, bank, taken = banks.take()
        token = None
        col_read = [None, None]
        for c in range(NC_F):
            made = step("vector", "bcol_made", lambda v, c=c: v.tensor_scalar(
                bcol[:, c % 2, :], ones[:], bv[:, c:c + 1], None, ALU.mult),
                [filled, bias_done["v"], col_read[c % 2]])

            def fold(pe, c=c, bank=bank):
                pe.matmul(bank[:, 0:D], bcol[:, c % 2, :], f32(wfc[:, HI, c, :]), start=(c == 0), stop=False)
                return pe.matmul(bank[:, 0:D], bcol[:, c % 2, :], f32(wfc[:, LO, c, :]), start=False,
                                 stop=(c == NC_F - 1))
            col_read[c % 2] = token = step("tensor", "bias_mm", fold, [made, weights, taken])
        fcb_ready = step("vector", "bias", lambda v, bank=bank: v.tensor_tensor(
            fcb[:], bank[:, 0:D], fcb[:], ALU.add), [token, consts])
        banks.give(index, fcb_ready)

        wo_t, wga = stage[0][:, 0:KD * D], stage[1][:, 0:KD * D]
        got = [load(f"raw{i}", lambda sp, dst=dst, src=src: sp.dma_start(
            dst.rearrange("p (k n) -> p k n", k=KD), src.rearrange("(k p) n -> p k n", p=P)), [stage_free[i]])
            for i, (dst, src) in enumerate(((wo_t, t["wo_t"]), (wga, t["wg"][0:D, :])))]
        for i in range(KD):
            index, bank, taken = banks.take()

            def wo_wg(pe, i=i, bank=bank):
                for k in range(KD):
                    last = pe.matmul(bank[:, 0:D], wo_t[:, k * D + i * P:k * D + (i + 1) * P],
                                     wga[:, k * D:(k + 1) * D], start=(k == 0), stop=(k == KD - 1))
                return last
            token = step("tensor", "bias_mm", wo_wg, got + [taken])
            done = step("vector", "bias", lambda v, i=i, bank=bank: v.tensor_copy(
                wog[:, i, D:2 * D], bank[:, 0:D]), [token])
            banks.give(index, done)
        index, bank, taken = banks.take()
        for k in range(KD):
            made = step("vector", "bcol_made", lambda v, k=k: v.tensor_scalar(
                bcol[:, k % 2, :], ones[:], bo_col[:, k:k + 1], None, ALU.mult), [col_read[k % 2], consts])
            token = step("tensor", "bias_mm", lambda pe, k=k, bank=bank: pe.matmul(
                bank[:, 0:D], bcol[:, k % 2, :], wga[:, k * D:(k + 1) * D], start=(k == 0), stop=(k == KD - 1)),
                [made, taken] + got)
        ready = step("vector", "bias", lambda v, bank=bank: v.tensor_tensor(
            bog[:, D:2 * D], bank[:, 0:D], bog[:, D:2 * D], ALU.add), [token, consts])
        banks.give(index, ready)
        hid_free, kblock_free = token, token

        setup = step("vector", "bias", lambda v: v.tensor_copy(
            wk1[:].rearrange("p k (j e) -> p k j e", j=HPC),
            wkv1[:, 0, :, :].unsqueeze(2).broadcast_to([P, KD, HPC, HD])), [consts])

        done = {}

        def of(stage, *index):
            return None if index[0] < 0 else done[stage, index]

        scratch_free = [None] * NT
        scratch_at = [0]
        soft_free, softT_free = [None] * NS, [None] * NS

        def layernorm_stats(tag, sources, st, mo, rs, after):
            n = len(sources)
            if True:
                def bn(v):
                    for i, src in enumerate(sources):
                        last = v.bn_stats(st[:, i, :], src)
                    return last
                a = step("vector", f"{tag}_stats", bn, after)

                def aggregate(v):
                    for i in range(n):
                        last = v.bn_aggr(mo[:, i, :], st[:, i, :])
                    return last
                a = step("vector", f"{tag}_stats", aggregate, [a])
                a = step("vector", f"{tag}_stats", lambda v: v.tensor_scalar(
                    rs[:, 0:n], mo[:, 0:n, 1], EPS0, None, ALU.add), [a])
            return step("gpsimd", f"{tag}_rstd", lambda p: p.tensor_tensor(
                rs[:, 0:n], rs[:, 0:n], half_exp[:, 0:n], ALU.pow), [a, filled])

        def normalise(tag, src, mo, rs, i, after):
            slot = scratch_at[0] % NT
            scratch_at[0] += 1
            token = step("vector", f"{tag}_norm", lambda v: v.tensor_scalar(
                normed[:, slot, :], src, mo[:, i, 0:1], rs[:, i:i + 1], ALU.subtract, ALU.mult),
                list(after) + [scratch_free[slot]])
            return slot, token

        def to_feature_major(tag, pieces, after):
            index, bank, taken = banks.take()
            view = bank[:].rearrange("p (k n) -> p k n", k=KD)

            def transposes(pe):
                for b, src in enumerate(pieces):
                    for k in range(KD):
                        last = pe.transpose(view[:, k, b * SEQ:(b + 1) * SEQ], src[:, k * P:(k + 1) * P], ident[:])
                return last
            token = step("tensor", f"{tag}_turned", transposes, list(after) + [taken, selected])
            return index, view, token

        def split_out(tag, bank_view, dst, token, free):
            hi = step("scalar", f"{tag}_hi", lambda a: a.copy(dst(HI), bank_view), [token] + list(free))
            return step("vector", f"{tag}_lo", lambda v: v.tensor_tensor(
                dst(LO), bank_view, f32(dst(HI)), ALU.subtract), [token, hi] + list(free))

        def fetch(g):
            s = g % 2
            done["x", (g,)] = load(f"load_x{s}", lambda sp: sp.dma_start(
                X[:, s, :, :], t["x"][g * GROUP:(g + 1) * GROUP].rearrange("b t d -> t b d")), [of("x1", g - 2)])
            done["c", (g,)] = load(f"load_c{s}", lambda sp: sp.dma_start(
                C[:, s, :, :], t["ctx"][g * GROUP:(g + 1) * GROUP].rearrange("b t d -> t b d")),
                [of("c_norm", g - 2), of("rawc_turned", g - 2)])

        def front_stats(g):
            s = g % 2
            done["ln", (g,)] = layernorm_stats(
                "ln0", [X[:, s, b, :] for b in range(GROUP)] + [C[:, s, b, :] for b in range(GROUP)],
                stats, moments, rstd, [of("x", g), of("c", g), of("x_norm", g - 1), of("c_norm", g - 1)])

        def front_norm(g, which):
            s, name, src, dst = g % 2, "xc"[which], (X, C)[which], (xT, cT)[which]
            pieces, tokens = [], []
            for b in range(GROUP):
                slot, token = normalise(name, src[:, s, b, :], moments, rstd, which * GROUP + b, [of("ln", g)])
                pieces.append((slot, normed[:, slot, :]))
                tokens.append(token)
            done[name + "_norm", (g,)] = tokens[-1]
            index, view, turned = to_feature_major(name, [x for _, x in pieces], tokens)
            for slot, _ in pieces:
                scratch_free[slot] = turned
            lo = split_out(name, view, lambda part: dst[:, part, :, :], turned, [of("proj_qk" if which == 0 else "proj_v", g - 1, NQ - 1),
                                                                               of("proj_qk", g - 1, NQ - 1)])
            banks.give(index, lo)
            done[name + "T", (g,)] = lo

        def front_raw(g):
            s = g % 2
            index, view, turned = to_feature_major("rawc", [C[:, s, b, :] for b in range(GROUP)], [of("c", g)])
            done["rawc_turned", (g,)] = turned
            raw = step("scalar", "rawc_copy", lambda a: a.copy(rawcT[:], view), [turned, of("proj_kv1", g - 1)])
            banks.give(index, raw)
            index, bank, taken = banks.take()

            def proj(pe):
                for k in range(KD):
                    pe.matmul(bank[:, 0:TOK], wk1[:, k, :], rawcT[:, k, :], start=(k == 0), stop=(k == KD - 1))
                for b in range(GROUP):
                    for k in range(KD):
                        last = pe.matmul(bank[:, TOK + b * HD:TOK + (b + 1) * HD], rawcT[:, k, b * SEQ:(b + 1) * SEQ],
                                         wkv1[:, 1, k, :], start=(k == 0), stop=(k == KD - 1))
                return last
            mm = done["proj_kv1", (g,)] = step("tensor", "proj_kv1", proj, [raw, taken, setup, consts])
            k1 = step("vector", "k1_out", lambda v: v.tensor_scalar(
                k1T[:, g % NK1, :], bank[:, 0:TOK], bk1[:, 0:1], None, ALU.add), [mm, of("kblock", g - NK1, GROUP - 1)])
            done["v1", (g,)] = step("vector", "k1_out", lambda v: v.tensor_tensor(
                v1[:, g % NK1, :, :], bank[:, TOK:TOK + GROUP * HD].rearrange("p (b e) -> p b e", b=GROUP),
                bv1[:].unsqueeze(1).broadcast_to([P, GROUP, HD]), ALU.add), [of("vpad", g - NK1, GROUP - 1)])
            banks.give(index, done["v1", (g,)])

        def proj_qk(g, Q):
            s = Q % 2
            for w, src, dst, bias, name in ((wq, xT, qT, bq, "q"), (wk, cT, kT, bk, "k")):
                index, bank, taken = banks.take()

                def mms(pe, w=w, src=src, bank=bank):
                    for c in range(QC):
                        cols = slice((Q * QC + c) * P, (Q * QC + c + 1) * P)
                        for k in range(KD):
                            last = mm3(pe, bank[:, c * TOK:(c + 1) * TOK], lambda part: w[:, part, k, cols],
                                       lambda part: src[:, part, k, :], k == 0, k == KD - 1)
                    return last
                mm = step("tensor", "proj_qk", mms, [of("xT", g), of("cT", g), taken, weights])
                free = of("scores", *(prev_unit(g, Q)))

                if name == "q":
                    def out(a, bank=bank):
                        for c in range(QC):
                            i = Q * QC + c
                            last = a.activation(qT[:, s, c, :], bank[:, c * TOK:(c + 1) * TOK], ACT.Identity,
                                                bias=bq[:, i:i + 1])
                        return last
                    token = step("scalar", "q_out", out, [mm, free, bias_done["q"]])
                else:
                    def out(v, bank=bank):
                        for c in range(QC):
                            i = Q * QC + c
                            last = v.tensor_scalar(kT[:, s, c, :], bank[:, c * TOK:(c + 1) * TOK], bk[:, i:i + 1],
                                                   None, ALU.add)
                        return last
                    token = step("vector", "k_out", out, [mm, free])
                banks.give(index, token)
                done[name, (g, Q)] = token
            done["proj_qk", (g, Q)] = mm

        def prev_unit(g, Q):
            n = g * NQ + Q - 2
            return (n // NQ, (n % NQ) * GROUP + GROUP - 1)

        def proj_v(g, Q):
            s = Q % 2
            index, bank, taken = banks.take()

            def mms(pe):
                for b in range(GROUP):
                    for k in range(KD):
                        last = mm3(pe, bank[:, b * QW:(b + 1) * QW], lambda part: cT[:, part, k, b * SEQ:(b + 1) * SEQ],
                                   lambda part: wv[:, part, k, Q * QW:(Q + 1) * QW], k == 0, k == KD - 1)
                return last
            mm = done["proj_v", (g, Q)] = step("tensor", "proj_v", mms, [of("cT", g), taken, weights])
            token = done["v", (g, Q)] = step("vector", "v_out", lambda v: v.tensor_copy(
                V[:, s, :, :].rearrange("p b n -> p (b n)"), bank[:]), [mm, of("pv", *prev_unit(g, Q))])
            banks.give(index, token)

        def softmax(tag, index, bank, bias_tile, scale, scored, slot):
            def biased_max(v):
                for h in range(QUAD):
                    last = v.tensor_tensor_reduce(soft[:, slot, h, :], bank[:, h * SEQ:(h + 1) * SEQ], bias_tile[:],
                                                  1.0, LOWEST, ALU.add, ALU.max, row_max[:, slot, h:h + 1])
                return last
            m = step("vector", "score_max", biased_max, [scored, soft_free[slot], consts, masks])
            banks.give(index, m)
            m = step("vector", "score_max", lambda v: v.tensor_scalar(
                neg_max[:, slot, :], row_max[:, slot, :], -scale, None, ALU.mult), [m])

            def exps(a):
                for h in range(QUAD):
                    last = a.activation(soft[:, slot, h, :], soft[:, slot, h, :], ACT.Exp,
                                        bias=neg_max[:, slot, h:h + 1], scale=scale,
                                        accum_out=row_sum[:, slot, h:h + 1])
                return last
            e = step("scalar", "exps", exps, [m])
            r = step("vector", "sum_inv", lambda v: v.reciprocal(inv_sum[:, slot, :], row_sum[:, slot, :]), [e])
            return step("gpsimd", "soft_norm", lambda p: p.tensor_tensor(
                soft[:, slot, :, :], soft[:, slot, :, :],
                inv_sum[:, slot, :].unsqueeze(2).broadcast_to([P, QUAD, SEQ]), ALU.mult), [e, r])

        def turn_probs(slot, normed_token, on_scalar):
            index, bank, taken = banks.take()

            def transposes(pe):
                for h in range(QUAD):
                    last = pe.transpose(bank[:, h * SEQ:(h + 1) * SEQ], soft[:, slot, h, :], ident[:])
                return last
            turned = step("tensor", "probs_turned", transposes, [normed_token, taken])
            soft_free[slot] = turned
            dst = softT[:, slot, :, :].rearrange("p h n -> p (h n)")
            if on_scalar:
                token = step("scalar", "probs_out_s", lambda a: a.copy(dst, bank[:]), [turned, softT_free[slot]])
            else:
                token = step("vector", "probs_out_v", lambda v: v.tensor_copy(dst, bank[:]), [turned, softT_free[slot]])
            banks.give(index, token)
            return token

        state = {}

        def tiles(m):
            return m // 2, m % 2 * HS, [(c, b) for c in range(QC) for b in range(GROUP)]

        def scores(g, m):
            Q, r, which = tiles(m)
            s = Q % 2
            index, bank, taken = banks.take()

            def mms(pe):
                for h, (c, b) in enumerate(which):
                    last = pe.matmul(bank[:, h * SEQ:(h + 1) * SEQ], qT[r:r + HS, s, c, b * SEQ:(b + 1) * SEQ],
                                     kT[r:r + HS, s, c, b * SEQ:(b + 1) * SEQ], start=True, stop=True)
                return last
            mm = done["scores", (g, m)] = step("tensor", "scores", mms, [of("q", g, Q), of("k", g, Q), taken])
            slot = m % 2
            token = softmax("a0", index, bank, relb, SCALE0, mm, slot)
            state["a0", g, m] = (slot, token)

        def turn0(g, m):
            slot, token = state["a0", g, m]
            state["a0", g, m] = (slot, turn_probs(slot, token, m % 2 == 0))

        def pv0(g, m):
            Q, r, which = tiles(m)
            s = Q % 2
            slot, token = state.pop(("a0", g, m))
            if r == 0:
                state["o0"] = banks.take()
            index, bank, taken = state["o0"]

            def mms(pe):
                for h, (c, b) in enumerate(which):
                    col = (b * QC + c) * SEQ
                    last = pe.matmul(bank[r:r + HS, col:col + SEQ], V[:, s, b, c * P + r:c * P + r + HS],
                                     softT[:, slot, h, :], start=True, stop=True)
                return last
            mm = done["pv", (g, m)] = step("tensor", "pv", mms, [token, of("v", g, Q), taken])
            softT_free[slot] = mm
            if r:
                dst = lambda part: OT[:, part, :, :, :].rearrange("p b c n -> p (b c n)")
                lo = split_out("o", bank[:], dst, mm, [state.get("fc_read")])
                banks.give(index, lo)
                state["oT"] = lo

        def fc(g, Q):
            if Q == 0:
                state["fc"] = banks.take()
            index, bank, taken = state["fc"]
            token = state["oT"]

            def mms(pe):
                for b in range(GROUP):
                    for c in range(QC):
                        last = mm3(pe, bank[:, b * D:(b + 1) * D], lambda part: OT[:, part, b, c, :],
                                   lambda part: wfc[:, part, Q * QC + c, :], Q == 0 and b == 0 and c == 0,
                                   Q == NQ - 1 and c == QC - 1, skip_group_check=True)
                return last
            state["fc_read"] = step("tensor", "fc", mms, [token, taken, weights])

        def finish_attention(g):
            s = g % 2
            index, bank, _ = state["fc"]
            xb = step("gpsimd", "x_plus_fcb", lambda p: p.tensor_tensor(
                X[:, s, :, :], X[:, s, :, :], fcb[:].unsqueeze(1).broadcast_to([P, GROUP, D]), ALU.add),
                [of("x", g), of("x_norm", g), fcb_ready])
            x1_done = done["x1", (g,)] = step("vector", "x1", lambda v: v.tensor_tensor(
                x1[:].rearrange("p b d -> p (b d)"), bank[:], X[:, s, :, :].rearrange("p b d -> p (b d)"), ALU.add),
                [state["fc_read"], xb, of("x1_read", g - 1)])
            banks.give(index, x1_done)
            rs = layernorm_stats("ln2", [x1[:, b, :] for b in range(GROUP)], stats2, moments2, rstd2, [x1_done])
            pieces, tokens = [], []
            for b in range(GROUP):
                slot, token = normalise("h", x1[:, b, :], moments2, rstd2, b, [rs])
                pieces.append(slot)
                tokens.append(token)
            done["x1b", (g,)] = step("gpsimd", "x1_plus_b2", lambda p: p.tensor_tensor(
                x1[:], x1[:], b2[:].unsqueeze(1).broadcast_to([P, GROUP, D]), ALU.add), [tokens[-1], consts])
            state["h", g] = (pieces, tokens)

        def turn_h(g):
            pieces, tokens = state.pop(("h", g))
            index, view, turned = to_feature_major("h", [normed[:, s, :] for s in pieces], tokens)
            for s in pieces:
                scratch_free[s] = turned
            lo = split_out("h", view, lambda part: hT[:, part, :, :], turned, [of("w1", g - 1, 1)])
            banks.give(index, lo)
            done["hT", (g,)] = lo

        def mlp_in(g, half, pair):
            index, bank, taken = banks.take()
            first = half * HH + pair * 2

            def mms(pe):
                for c in range(2):
                    for k in range(KD):
                        last = mm3(pe, bank[:, c * TOK:(c + 1) * TOK],
                                   lambda part: w1[:, part, k, (first + c) * P:(first + c + 1) * P],
                                   lambda part: hT[:, part, k, :], k == 0, k == KD - 1)
                return last
            mm = done["w1", (g, half)] = step("tensor", "w1", mms, [of("hT", g), taken, weights])

            def out(a):
                for c in range(2):
                    last = a.activation(hid[:, pair * 2 + c, :], bank[:, c * TOK:(c + 1) * TOK], ACT.Identity,
                                        bias=b1[:, first + c:first + c + 1])
                return last
            token = step("scalar", "hid_out", out, [mm, state.get("hid_read", hid_free), bias_done["1"]])
            banks.give(index, token)
            state["hid"] = token

        def gelu(g, half):
            flat = hid[:].rearrange("p c n -> p (c n)")
            act = step("scalar", "gelu", lambda a: a.activation(flat, flat, ACT.Gelu), [state["hid"]])
            hi = step("vector", "hid_hi", lambda v: v.tensor_copy(
                hidS[:, HI, :, :].rearrange("p c n -> p (c n)"), flat), [act, state.get("w2_read")])
            lo = step("gpsimd", "hid_lo", lambda p: p.tensor_tensor(
                hidS[:, LO, :, :].rearrange("p c n -> p (c n)"), flat,
                f32(hidS[:, HI, :, :]).rearrange("p c n -> p (c n)"), ALU.subtract), [hi, act])
            state["hid_read"] = lo
            state["hidS"] = lo

        def mlp_out(g, half, b):
            if half == 0 and b == 0:
                state["w2"] = banks.take()
            index, bank, taken = state["w2"]

            def mms(pe):
                for c in range(HH):
                    last = mm3(pe, bank[:, b * D:(b + 1) * D], lambda part: hidS[:, part, c, b * SEQ:(b + 1) * SEQ],
                               lambda part: w2[:, part, half * HH + c, :], half == 0 and b == 0 and c == 0,
                               half == 1 and c == HH - 1, skip_group_check=True)
                return last
            state["w2_read"] = step("tensor", "w2", mms, [state["hidS"], taken, weights])

        def block1_in(g):
            index, bank, _ = state["w2"]
            flat = x1[:].rearrange("p b d -> p (b d)")
            x2 = done["x2", (g,)] = step("vector", "x2", lambda v: v.tensor_tensor(flat, bank[:], flat, ALU.add),
                                         [state["w2_read"], of("x1b", g)])
            banks.give(index, x2)

        def turn_x2(g):
            index, view, turned = to_feature_major("x2", [x1[:, b, :] for b in range(GROUP)], [of("x2", g)])
            token = done["x2T", (g,)] = step("scalar", "x2_out", lambda a: a.copy(x2T[:], view),
                                             [turned, of("out_mm", g - 1, GROUP - 1)])
            banks.give(index, token)

        def proj_q1(g):
            index, bank, taken = banks.take()

            def mms(pe):
                for c in range(KD):
                    for k in range(KD):
                        last = pe.matmul(bank[:, c * TOK:(c + 1) * TOK], wq1[:, k, c * P:(c + 1) * P], x2T[:, k, :],
                                         start=(k == 0), stop=(k == KD - 1))
                return last
            mm = step("tensor", "proj_q1", mms, [of("x2T", g), taken, consts])

            def out(a):
                for c in range(KD):
                    last = a.activation(q1T[:, c, :], bank[:, c * TOK:(c + 1) * TOK], ACT.Identity,
                                        bias=bq1[:, c:c + 1])
                return last
            token = done["q1", (g,)] = step("scalar", "q1_out", out, [mm, of("scores1", g - 1, GROUP - 1, NU1 - 1)])
            banks.give(index, token)

        def spread_kv(g, b):
            s = g % NK1
            pg, pb = (g, b - 1) if b else (g - 1, GROUP - 1)
            done["kblock", (g, b)] = step("gpsimd", "kblock", lambda p: p.tensor_tensor(
                kblock[:], k1T[:, s, b * SEQ:(b + 1) * SEQ].unsqueeze(1).broadcast_to([P, HPC, SEQ]),
                block_of[:].unsqueeze(2).broadcast_to([P, HPC, SEQ]), ALU.mult),
                [of("v1", g), of("scores1", pg, pb, NU1 - 1) or kblock_free, masks])
            done["vpad", (g, b)] = step("gpsimd", "vpad", lambda p: p.tensor_copy(
                vpad[:].rearrange("p (j n) -> p j n", n=VSTEP)[:, :, 0:HD],
                v1[:, s, b, :].unsqueeze(1).broadcast_to([P, HPC, HD])),
                [of("v1", g), of("pv1", pg, pb, NU1 - 1), filled])

        def scores1(g, b, u):
            index, bank, taken = banks.take()
            c, j = u * QUAD // HPC, u * QUAD % HPC
            mm = done["scores1", (g, b, u)] = step("tensor", "scores1", lambda pe: pe.matmul(
                bank[:], q1T[:, c, b * SEQ:(b + 1) * SEQ], kblock[:, j:j + QUAD, :], start=True, stop=True),
                [of("q1", g), of("kblock", g, b), taken])
            slot = 2 + u % 2
            state["a1", g, b, u] = (slot, softmax("a1", index, bank, winb, SCALE1, mm, slot))

        def turn1(g, b, u):
            slot, token = state["a1", g, b, u]
            state["a1", g, b, u] = (slot, turn_probs(slot, token, u % 2 == 1))

        def pv1(g, b, u):
            slot, token = state.pop(("a1", g, b, u))
            if u == 0:
                state["o1"] = banks.take()
            index, bank, taken = state["o1"]
            c, j = u * QUAD // HPC, u * QUAD % HPC

            def mms(pe):
                for h in range(QUAD):
                    last = pe.matmul(bank[:, c * SEQ:(c + 1) * SEQ], vpad[:, (j + h) * P:(j + h + 1) * P],
                                     softT[:, slot, h, :], start=(j + h == 0), stop=(j + h == HPC - 1))
                return last
            mm = done["pv1", (g, b, u)] = step("tensor", "pv1", mms, [token, of("vpad", g, b), taken])
            softT_free[slot] = mm
            if u == NU1 - 1:
                pg, pb = (g, b - 1) if b else (g - 1, GROUP - 1)
                token = done["o1", (g, b)] = step("vector", "o1_out", lambda v: v.tensor_copy(
                    o1T[:].rearrange("p c n -> p (c n)"), bank[:, 0:KD * SEQ]), [mm, of("out_mm", pg, pb)])
                banks.give(index, token)

        def out_mm(g, b):
            index, bank, taken = banks.take()

            def mms(pe):
                pe.matmul(bank[:], o1T[:, 0, :], wog[:, 0, :], start=True, stop=False)
                for k in range(KD):
                    pe.matmul(bank[:, D:2 * D], x2T[:, k, b * SEQ:(b + 1) * SEQ], wgx[:, k, :],
                              start=False, stop=False, skip_group_check=True)
                return pe.matmul(bank[:], o1T[:, 1, :], wog[:, 1, :], start=False, stop=True)
            mm = done["out_mm", (g, b)] = step("tensor", "out_mm", mms, [of("o1", g, b), of("x2T", g), taken, setup])
            pg, pb = (g, b - 1) if b else (g - 1, GROUP - 1)
            a0 = step("vector", "ag", lambda v: v.tensor_tensor(ag[:], bank[:], bog[:], ALU.add),
                      [mm, of("mix1", pg, pb), ready])
            banks.give(index, a0)
            th = step("scalar", "tanh", lambda a: a.activation(gate[:], ag[:, D:2 * D], ACT.Tanh, scale=0.5),
                      [a0, of("mix1", pg, pb)])
            df = step("gpsimd", "mix", lambda p: p.tensor_tensor(ag[:, 0:D], ag[:, 0:D], x1[:, b, :], ALU.subtract),
                      [a0, of("mix2", pg, pb)])
            g1 = step("vector", "gate", lambda v: v.tensor_scalar(gate[:], gate[:], 0.5, 0.5, ALU.mult, ALU.add), [th])
            g2 = step("gpsimd", "mix", lambda p: p.tensor_tensor(gate[:], gate[:], ag[:, D:2 * D], ALU.mult), [g1])
            m1 = done["mix1", (g, b)] = step("gpsimd", "mix", lambda p: p.tensor_tensor(
                ag[:, 0:D], ag[:, 0:D], gate[:], ALU.mult), [g2, df])
            m2 = done["mix2", (g, b)] = step("gpsimd", "mix", lambda p: p.tensor_tensor(
                mixed[:], ag[:, 0:D], x1[:, b, :], ALU.add), [m1, of("mix_read", pg, pb)])
            if b == GROUP - 1:
                done["x1_read", (g,)] = m2
            sq = step("scalar", "square", lambda a: a.activation(gate[:], mixed[:], ACT.Square,
                                                                 accum_out=sumsq[:, 0:1]), [m2])
            done["mix1", (g, b)] = sq
            ms = step("vector", "gate", lambda v: v.tensor_scalar(
                rrms[:], sumsq[:], 1.0 / D, EPS1, ALU.mult, ALU.add), [sq, of("mix_read", pg, pb)])
            rr = step("gpsimd", "rrms", lambda p: p.tensor_tensor(rrms[:], rrms[:], half_exp[:, 0:1], ALU.pow), [ms])
            pc = of("center", pg, pb)
            xh = step("vector", "x_hat", lambda v: v.scalar_tensor_tensor(
                mixed[:], mixed[:], rrms[:, 0:1], rmsw[:], ALU.mult, ALU.mult), [rr, sq, m2, pc])
            state["xhat", g, b] = xh

        def center_out(g, b):
            xh = state.pop(("xhat", g, b))
            index, bank, taken = banks.take()
            mm = done["center", (g, b)] = step("tensor", "center", lambda pe: pe.matmul(
                bank[:, 0:D], center[:], mixed[:], start=True, stop=True), [xh, taken, selected])
            done["mix_read", (g, b)] = mm
            n = g * GROUP + b
            y = step("scalar", "y_out", lambda a: a.copy(Y[:], bank[:, 0:D]), [mm, of("stored", n - 1)])
            banks.give(index, y)
            done["stored", (n,)] = load("store", lambda sp: sp.dma_start(t["out"][n], Y[:]), [y])

        def stream_two(g):
            pieces = [lambda: turn_h(g), lambda: mlp_in(g, 0, 0), lambda: mlp_in(g, 0, 1),
                      lambda: (gelu(g, 0), spread_kv(g, 0)), lambda: mlp_in(g, 1, 0), lambda: mlp_in(g, 1, 1),
                      lambda: mlp_out(g, 0, 0), lambda: mlp_out(g, 0, 1), lambda: gelu(g, 1),
                      lambda: mlp_out(g, 1, 0), lambda: mlp_out(g, 1, 1),
                      lambda: block1_in(g), lambda: turn_x2(g), lambda: proj_q1(g)]
            units = [(b, u) for b in range(GROUP) for u in range(NU1)]
            for n in range(len(units) + 4):
                if n < len(units):
                    pieces.append(lambda b=units[n][0], u=units[n][1]: scores1(g, b, u))
                if n < len(units) and units[n] == (0, NU1 - 1):
                    pieces.append(lambda: spread_k_next(g))
                if 1 <= n <= len(units):
                    pieces.append(lambda b=units[n - 1][0], u=units[n - 1][1]: turn1(g, b, u))
                if 2 <= n <= len(units) + 1:
                    pieces.append(lambda b=units[n - 2][0], u=units[n - 2][1]: pv1(g, b, u))
                    if units[n - 2][1] == NU1 - 1:
                        pieces.append(lambda b=units[n - 2][0]: out_mm(g, b))
                        if units[n - 2][0] == 0:
                            pieces.append(lambda: None)
                if n >= 4 and units[n - 4][1] == NU1 - 1:
                    pieces.append(lambda b=units[n - 4][0]: center_out(g, b))
            return pieces

        def spread_k_next(g):
            s = g % NK1
            b = 1
            done["kblock", (g, b)] = step("gpsimd", "kblock", lambda p: p.tensor_tensor(
                kblock[:], k1T[:, s, b * SEQ:(b + 1) * SEQ].unsqueeze(1).broadcast_to([P, HPC, SEQ]),
                block_of[:].unsqueeze(2).broadcast_to([P, HPC, SEQ]), ALU.mult),
                [of("scores1", g, 0, NU1 - 1)])

        pv1_plain = pv1

        def pv1(g, b, u):
            if b == 1 and u == 0:
                s = g % NK1
                done["vpad", (g, 1)] = step("gpsimd", "vpad", lambda p: p.tensor_copy(
                    vpad[:].rearrange("p (j n) -> p j n", n=VSTEP)[:, :, 0:HD],
                    v1[:, s, 1, :].unsqueeze(1).broadcast_to([P, HPC, HD])), [of("pv1", g, 0, NU1 - 1)])
            pv1_plain(g, b, u)

        backlog = []
        UNITS = NQ * GROUP

        def drain():
            while backlog:
                backlog.pop(0)()

        def step_pieces(n):
            g, m = n // UNITS, n % UNITS
            pieces = []
            if n < NG * UNITS:
                pieces.append(lambda: scores(g, m))
            if 2 <= n and n - 2 < NG * UNITS:
                pieces.append(lambda: pv0((n - 2) // UNITS, (n - 2) % UNITS))
            if 1 <= n and n - 1 < NG * UNITS:
                pieces.append(lambda: turn0((n - 1) // UNITS, (n - 1) % UNITS))
            if g < NG:
                ng, nq = (g, m // GROUP + 1) if m // GROUP + 1 < NQ else (g + 1, 0)
                if m == 3 and g + 1 < NG:
                    pieces.append(lambda: fetch(g + 1))
                if m == 5 and g + 1 < NG:
                    pieces.append(lambda: front_stats(g + 1))
                if ng < NG and m % GROUP == 0:
                    if m == UNITS - 2:
                        pieces += [lambda: front_norm(g + 1, 0), lambda: front_norm(g + 1, 1)]
                    pieces.append(lambda: proj_qk(ng, nq))
                if ng < NG and m % GROUP == 1:
                    if m == UNITS - 1:
                        pieces.append(lambda: front_raw(g + 1))
                    pieces.append(lambda: proj_v(ng, nq))
            k = n - 3
            if k >= 0 and k % GROUP == GROUP - 1 and k < NG * UNITS:
                kg, kq = k // UNITS, (k % UNITS) // GROUP
                pieces.append(lambda: fc(kg, kq))
                if kq == NQ - 1:
                    pieces.append(lambda: (drain(), finish_attention(kg)))
                    pieces.append(lambda: backlog.extend(stream_two(kg)))
            return pieces

        fetch(0)
        front_stats(0)
        front_norm(0, 0)
        front_norm(0, 1)
        front_raw(0)
        proj_qk(0, 0)
        proj_v(0, 0)
        per_step = -(-len(stream_two(0)) // UNITS)
        n = 0
        while n < NG * UNITS + 4 or backlog:
            one = step_pieces(n) if n < NG * UNITS + 4 else []
            n_two = min(per_step, len(backlog))
            total = max(len(one), n_two)
            i = j = 0
            for r in range(1, total + 1):
                while i < r * len(one) // total:
                    one[i]()
                    i += 1
                while backlog and j < r * n_two // total:
                    backlog.pop(0)()
                    j += 1
            n += 1
        name, value = done["stored", (NBATCH - 1,)]
        fin = [(S.sem[name], value)]

        block = ctx.enter_context(nc.Block())

        @block.sync
        def _(eng):
            S.replay("sync", eng)
            for sem, value in fin:
                eng.wait_ge(sem, value)

        @block.tensor
        def _(eng):
            S.replay("tensor", eng)

        @block.vector
        def _(eng):
            S.replay("vector", eng)

        @block.scalar
        def _(eng):
            S.replay("scalar", eng)

        @block.gpsimd
        def _(eng):
            S.replay("gpsimd", eng)


def kernel(x, ctx_1024, **w):
    import concourse.bacc as bacc
    from concourse.bass_utils import run_bass_kernel_spmd

    D = x.shape[2]
    T = x.shape[1]
    a = {k.replace("L0_xattn_", "0").replace("L1_xattn_", "1"): v for k, v in w.items()}
    rel = a["0rel_bias"]
    ntok = (rel.shape[0] + 1) // 2


    def columns(v):
        return v.reshape(-1, P).T

    arrays = {
        "x": x, "ctx": ctx_1024,
        "wq_t": a["0Wq"].reshape(-1, D).T, "wk_t": a["0Wk"].reshape(-1, D).T, "wv_t": a["0Wv"].reshape(-1, D).T,
        "fc_t": a["0fc_w"].T, "w1_t": a["0W1"].T, "w2_t": a["0W2"].T,
        "ln_q_g": columns(a["0ln_q_g"]), "ln_q_b": columns(a["0ln_q_b"]), "ln_k_g": columns(a["0ln_k_g"]), "ln_k_b": columns(a["0ln_k_b"]),
        "ln_v_g": columns(a["0ln_v_g"]), "ln_v_b": columns(a["0ln_v_b"]), "ln2_g": columns(a["0ln2_g"]), "ln2_b": columns(a["0ln2_b"]),
        "fc_b": a["0fc_b"], "b1": columns(a["0b1"]), "b2": a["0b2"],
        "rel": np.stack([rel[r + ntok - T:r + ntok][::-1] for r in range(T)]),
        "wq1": a["1Wq"], "wk1": a["1Wk"], "wv1": a["1Wv"], "bq1": columns(a["1bq"]), "bk1": a["1bk"], "bv1": a["1bv"],
        "wo": a["1Wo"], "wo_t": a["1Wo"].T, "bo": a["1bo"], "bo_col": columns(a["1bo"]), "wg": a["1Wg"], "bg": a["1bg"], "rms_w": a["1rms_w"],
    }
    nc = bacc.Bacc("TRN2", target_bir_lowering=False, num_devices=1)
    ins, tensors = {}, {}
    for name, v in arrays.items():
        v = np.ascontiguousarray(v)
        ins[f"in_{name}"] = v
        tensors[name] = nc.dram_tensor(f"in_{name}", v.shape, mybir.dt.from_np(v.dtype), kind="ExternalInput").ap()
    tensors["out"] = nc.dram_tensor("out_0", x.shape, F32, kind="ExternalOutput").ap()
    two_block_xattn(nc, tensors)
    r = run_bass_kernel_spmd(nc, [ins], core_ids=[0])
    return r.results[0]["out_0"]
```

```python
from contextlib import ExitStack

import numpy as np

import concourse.bass as bass
from concourse import mybir

F32 = mybir.dt.float32
F32R = mybir.dt.float32r
ALU = mybir.AluOpType
ACT = mybir.ActivationFunctionType

P = 128
HI, LO = 0, 1
BANKS, BANK = 8, 512


class Steps:

    ENGINES = ("sync", "tensor", "vector", "scalar", "gpsimd")

    LENGTH = dict(x_turned=0.5, c_turned=0.5, rawc_turned=0.5, h_turned=0.5, x2_turned=0.5, proj_qk=1.35,
                  proj_v=1.35, proj_kv1=1.3, proj_q1=1.8, scores=1.0, scores1=0.9, probs0_turned=0.45,
                  probs1_turned=0.45, pv=0.65, pv1=0.95, fc=1.35, w1=1.35, w2=1.35, out_mm=2.6, center=0.45,
                  score_max=0.5, sum_inv=0.1, k_out=0.8, v_out=0.6, probs_out_v=0.6, o_lo=0.6, x_lo=0.6, c_lo=0.6,
                  h_lo=0.6, hid_hi=0.6, hid_lo=1.15, o1_out=0.35, k1_out=0.3, ag=0.6, gate=0.2, x_hat=0.4, x1=0.6,
                  x2=0.6, ln0_stats=0.6, ln2_stats=0.35, x_norm=0.33, c_norm=0.33, h_norm=0.33,
                  exps=1.7, q_out=0.72, probs_out_s=0.5, o_hi=0.5, x_hi=0.5, c_hi=0.5, h_hi=0.5, hid_out=0.72,
                  gelu=3.8, q1_out=0.72, x2_out=0.5, rawc_copy=0.5, tanh=0.4, square=0.5, y_out=0.3,
                  norm_a0=1.1, norm_a1=1.1, kblock=1.0, vpad=0.6, mix=0.7, rrms=0.5, ln0_rstd=1.0, ln2_rstd=0.7,
                  x_plus_fcb=1.3, x1_plus_b2=1.3, load_x0=2.5, load_x1=2.5, load_c=2.5, store=2.5)
    HANDOVER = 0.15

    def __init__(self, nc, ctx):
        self.clock = {e: 0.0 for e in self.ENGINES}
        self.ends = {}
        self.nc, self.ctx = nc, ctx
        self.queue = {e: [] for e in self.ENGINES}
        self.sem, self.count, self.engine_of = {}, {}, {}
        self.passed = {e: {} for e in self.ENGINES}

    def step(self, engine, name, work, after=(), by=1):
        if name not in self.sem:
            self.sem[name] = self.ctx.enter_context(self.nc.semaphore(name))
            self.count[name], self.engine_of[name] = 0, engine
        assert self.engine_of[name] == engine
        waits = []
        for token in after:
            if token is None:
                continue
            other, value = token
            if self.passed[engine].get(other, 0) < value:
                self.passed[engine][other] = value
                waits.append((self.sem[other], value))
        self.count[name] += by
        self.queue[engine].append((waits, work, self.sem[name], by))
        length = self.LENGTH.get(name, 1.0)
        end = max(self.clock[engine], self.reached(after)) + length
        self.clock[engine] = end if engine != "sync" else self.clock[engine]
        self.ends[name, self.count[name]] = end + self.HANDOVER
        return name, self.count[name]

    def reached(self, tokens):
        return max((self.ends.get(token, 0.0) for token in tokens), default=0.0)

    def load(self, name, work, after=()):
        return self.step("sync", name, work, after, by=16)

    def replay(self, engine, eng):
        for waits, work, sem, by in self.queue[engine]:
            for other, value in waits:
                eng.wait_ge(other, value)
            work(eng).then_inc(sem, by)


class Banks:

    def __init__(self, tiles):
        self.tiles, self.free = tiles, [(i, None) for i in range(len(tiles))]

    def take(self):
        index, token = self.free.pop(0)
        return index, self.tiles[index], token

    def give(self, index, token):
        self.free.append((index, token))

    def next_token(self):
        return self.free[0][1]


def two_block_xattn(nc, t):
    NBATCH, SEQ, D = t["x"].shape
    GROUP = 2
    NG = NBATCH // GROUP
    KD = D // P
    TOK = GROUP * SEQ
    F = t["wq_t"].shape[1]
    H0 = 16
    HS = F // H0
    NC_F = F // P
    QUAD = BANK // SEQ
    NQ = H0 // QUAD
    QC = QUAD * HS // P
    QW = QUAD * HS
    H1 = 16
    HD = D // H1
    HPC = P // HD
    NU1 = H1 // QUAD
    WINDOW_HALF = 64
    EPS0, EPS1 = 1e-5, 1e-6
    SCALE0, SCALE1 = float(HS) ** -0.5, float(HD) ** -0.5
    MASKED = -1e30
    LOWEST = -3.0e38
    assert SEQ == P and D == 256

    with ExitStack() as ctx:
        S = Steps(nc, ctx)
        step, load = S.step, S.load

        def sb(name, shape, dt=F32):
            return ctx.enter_context(nc.sbuf_tensor(name, shape, dt))

        banks = Banks([ctx.enter_context(nc.psum_tensor(f"bank{i}", [P, BANK], F32)) for i in range(BANKS)])

        wq = sb("wq", [P, 2, KD, F], F32R)
        wk = sb("wk", [P, 2, KD, F], F32R)
        wv = sb("wv", [P, 2, KD, F], F32R)
        wfc = sb("wfc", [P, 2, NC_F, D], F32R)
        w1 = sb("w1", [P, 2, KD, F], F32R)
        w2 = sb("w2", [P, 2, NC_F, D], F32R)
        wq1 = sb("wq1", [P, KD, D])
        wkv1 = sb("wkv1", [P, 2, KD, HD])
        wk1 = sb("wk1", [P, KD, P])
        wog = sb("wog", [P, KD, 2 * D])
        wgx = sb("wgx", [P, KD, D])
        gains = sb("gains", [P, 3 + 1, KD])
        shifts = sb("shifts", [P, 3 + 1, KD])
        ident = sb("ident", [P, P])
        center = sb("center", [P, P])
        relb = sb("relb", [P, SEQ])
        winb = sb("winb", [P, SEQ])
        block_of = sb("block_of", [P, HPC])
        ones = sb("ones", [P, P])
        half_exp = sb("half_exp", [P, 4])
        bq = sb("bq", [P, NC_F])
        bk = sb("bk", [P, NC_F])
        bv = sb("bv", [P, NC_F])
        b1 = sb("b1", [P, NC_F])
        bq1 = sb("bq1", [P, KD])
        bk1 = sb("bk1", [P, 1])
        bo_col = sb("bo_col", [P, KD])
        fcb = sb("fcb", [P, D])
        b2 = sb("b2", [P, D])
        bog = sb("bog", [P, 2 * D])
        bv1 = sb("bv1", [P, HD])
        rmsw = sb("rmsw", [P, D])
        X = sb("X", [P, 2, GROUP, D])
        C = sb("C", [P, GROUP, D])
        NT = 4
        normed = sb("normed", [P, NT, D])
        stats = sb("stats", [P, 4, 6])
        moments = sb("moments", [P, 4, 2])
        rstd = sb("rstd", [P, 4])
        stats2 = sb("stats2", [P, GROUP, 6])
        moments2 = sb("moments2", [P, GROUP, 2])
        rstd2 = sb("rstd2", [P, GROUP])
        xT = sb("xT", [P, 2, KD, TOK], F32R)
        cT = sb("cT", [P, 2, KD, TOK], F32R)
        hT = sb("hT", [P, 2, KD, TOK], F32R)
        rawcT = sb("rawcT", [P, KD, TOK])
        qT = sb("qT", [P, 2, QC, TOK])
        kT = sb("kT", [P, 2, QC, TOK])
        V = sb("V", [P, 2, GROUP, QW])
        OT = sb("OT", [P, 2, GROUP, QC, SEQ], F32R)
        NS = 4
        soft = sb("soft", [P, NS, QUAD, SEQ])
        softT = sb("softT", [P, NS, QUAD, SEQ])
        row_max = sb("row_max", [P, NS, QUAD])
        neg_max = sb("neg_max", [P, NS, QUAD])
        row_sum = sb("row_sum", [P, NS, QUAD])
        inv_sum = sb("inv_sum", [P, NS, QUAD])
        x1 = sb("x1", [P, 2, GROUP, D])
        HH = NC_F // 2
        hid = sb("hid", [P, HH, TOK])
        hidS = sb("hidS", [P, 2, HH, TOK], F32R)
        x2T = sb("x2T", [P, KD, TOK])
        q1T = sb("q1T", [P, KD, TOK])
        NK1 = 3
        k1T = sb("k1T", [P, NK1, TOK])
        v1 = sb("v1", [P, NK1, GROUP, HD])
        kblock = sb("kblock", [P, HPC, SEQ])
        VSTEP = P + HD
        vpad = sb("vpad", [P, HPC * VSTEP])
        o1T = sb("o1T", [P, KD, SEQ])
        ag = sb("ag", [P, 2 * D])
        gate = sb("gate", [P, D])
        mixed = sb("mixed", [P, D])
        sumsq = sb("sumsq", [P, 1])
        rrms = sb("rrms", [P, 1])
        Y = sb("Y", [P, D])

        def f32(ap):
            return ap.bitcast(F32)

        def mm3(pe, out, stat, mov, first, last, **kw):
            pe.matmul(out, stat(LO), mov(HI), start=first, stop=False, **kw)
            pe.matmul(out, stat(HI), mov(LO), start=False, stop=False, **kw)
            return pe.matmul(out, stat(HI), mov(HI), start=False, stop=last, **kw)

        def bcast(ap):
            return ap.partition_broadcast(P)

        small = []
        for i, n in enumerate(("ln_q", "ln_k", "ln_v", "ln2")):
            small.append((gains[:, i, :], t[n + "_g"]))
            small.append((shifts[:, i, :], t[n + "_b"]))
        small += [(relb[:], t["rel"]), (fcb[:], bcast(t["fc_b"])), (b2[:], bcast(t["b2"])),
                  (b1[:], t["b1"]), (bq1[:], t["bq1"]), (bo_col[:], t["bo_col"]),
                  (bog[:, 0:D], bcast(t["bo"])), (bog[:, D:2 * D], bcast(t["bg"])),
                  (bv1[:], bcast(t["bv1"])), (rmsw[:], bcast(t["rms_w"])),
                  (wq1[:], t["wq1"].rearrange("(k p) n -> p k n", p=P)),
                  (wkv1[:, 0, :, :], t["wk1"].rearrange("(k p) n -> p k n", p=P)),
                  (wkv1[:, 1, :, :], t["wv1"].rearrange("(k p) n -> p k n", p=P)),
                  (wog[:, :, 0:D], t["wo"].rearrange("(k p) n -> p k n", p=P)),
                  (wgx[:], t["wg"][D:2 * D, :].rearrange("(k p) n -> p k n", p=P))]
        small += [(bk1[HD * j:HD * (j + 1), :], t["bk1"].rearrange("(p o) -> p o", o=1)) for j in range(HPC)]

        def load_small(sp):
            for dst, src in small[:-1]:
                sp.dma_start(dst, src).then_inc(S.sem["consts"], 16)
            return sp.dma_start(*small[-1])
        S.sem["consts"] = ctx.enter_context(nc.semaphore("consts"))
        S.count["consts"], S.engine_of["consts"] = 16 * (len(small) - 1), "sync"
        consts = load("consts", load_small)

        def pool_consts(pool):
            pool.memset(half_exp[:], -0.5)
            pool.memset(ones[:], 1.0)
            pool.memset(ident[:], 0.0)
            pool.memset(center[:], -1.0 / SEQ)
            pool.memset(winb[:], 0.0)
            pool.memset(block_of[:], 1.0)
            return pool.memset(vpad[:], 0.0)
        filled = step("gpsimd", "filled", pool_consts)

        def pool_select(pool):
            pool.affine_select(out=ident[:], in_=ident[:], compare_op=ALU.not_equal, fill=1.0, base=0,
                               pattern=[[-1, P]], channel_multiplier=1)
            pool.affine_select(out=center[:], in_=center[:], compare_op=ALU.not_equal, fill=1.0 - 1.0 / SEQ,
                               base=0, pattern=[[-1, P]], channel_multiplier=1)
            pool.affine_select(out=winb[:], in_=winb[:], compare_op=ALU.is_ge, fill=MASKED,
                               base=WINDOW_HALF, pattern=[[1, SEQ]], channel_multiplier=-1)
            return pool.affine_select(out=block_of[:], in_=block_of[:], compare_op=ALU.is_ge, fill=0.0, base=0,
                                      pattern=[[-HD, HPC]], channel_multiplier=1)
        selected = step("gpsimd", "selected", pool_select, [filled])

        def pool_select2(pool):
            pool.affine_select(out=winb[:], in_=winb[:], compare_op=ALU.is_ge, fill=MASKED,
                               base=WINDOW_HALF, pattern=[[-1, SEQ]], channel_multiplier=1)
            return pool.affine_select(out=block_of[:], in_=block_of[:], compare_op=ALU.is_ge, fill=0.0,
                                      base=HD - 1, pattern=[[HD, HPC]], channel_multiplier=-1)
        masks = step("gpsimd", "selected", pool_select2, [selected])

        stage = [hid[:].rearrange("p a b -> p (a b)"), kblock[:].rearrange("p a b -> p (a b)")]
        stage_free = [None, None]
        HALF = KD * F // 2
        bias_done = {}

        def prepare(n, name, src, dst, gain, bias_cols):
            slot = prepare.count % 2
            prepare.count += 1
            buf = stage[slot]
            raw = load(f"raw{slot}", lambda sp: sp.dma_start(
                buf if len(src.shape) == 2 else buf.rearrange("p (c n) -> p c n", c=src.shape[1]), src),
                [stage_free[slot]])
            used = None
            if bias_cols is not None:
                shift, out_bank, taken = bias_cols

                def bias_mm(pe):
                    for c in range(NC_F):
                        last = pe.matmul(out_bank[:, c:c + 1], buf[:, c * P:(c + 1) * P], shifts[:, shift, n:n + 1],
                                         start=(n == 0 and c == 0), stop=(n == KD - 1), skip_group_check=True)
                    return last
                used = step("tensor", "bias_mm", bias_mm, [raw, consts, taken])
                bias_done[name] = used
            ready = raw
            if gain is not None:
                ready = step("vector", "scaled", lambda v: v.tensor_scalar(
                    buf, buf, gains[:, gain, n:n + 1], None, ALU.mult), [raw, consts, used])
            hi = step("scalar", "w_hi", lambda a: a.copy(dst(HI), buf), [ready])
            lo = step("vector", "w_lo", lambda v: v.tensor_tensor(dst(LO), buf, f32(dst(HI)), ALU.subtract),
                      [ready, hi])
            stage_free[slot] = lo
            return lo
        prepare.count = 0

        def half_k(w):
            return lambda n: (lambda part: w[:, part, n, :])

        def half_c(w):
            half = NC_F // 2
            return lambda n: (lambda part: w[:, part, n * half:(n + 1) * half, :].rearrange("p c n -> p (c n)"))

        for name, w, idx, src, bias in (("q", wq, 0, "wq_t", bq), ("k", wk, 1, "wk_t", bk), ("v", wv, 2, "wv_t", bv),
                                        ("1", w1, 3, "w1_t", b1)):
            index, bank, taken = banks.take()
            for n in range(KD):
                prepare(n, name, t[src][n * P:(n + 1) * P, :], half_k(w)(n), idx, (idx, bank, taken))
            if name == "1":
                done = step("vector", "bias", lambda v, bank=bank: v.tensor_tensor(
                    b1[:], bank[:, 0:NC_F], b1[:], ALU.add), [bias_done[name], consts])
            else:
                done = step("vector", "bias", lambda v, bank=bank, bias=bias: v.tensor_copy(
                    bias[:], bank[:, 0:NC_F]), [bias_done[name]])
            banks.give(index, done)
            bias_done[name] = done
        for w, src in ((wfc, "fc_t"), (w2, "w2_t")):
            for n in range(2):
                rows = F // 2
                weights = prepare(n, src, t[src][n * rows:(n + 1) * rows, :].rearrange("(c p) n -> p c n", p=P),
                                  half_c(w)(n), None, None)

        bcol = x1[:, 0, :, 0:P]
        index, bank, taken = banks.take()
        token = None
        col_read = [None, None]
        for c in range(NC_F):
            made = step("vector", "bcol_made", lambda v, c=c: v.tensor_scalar(
                bcol[:, c % 2, :], ones[:], bv[:, c:c + 1], None, ALU.mult),
                [filled, bias_done["v"], col_read[c % 2]])

            def fold(pe, c=c, bank=bank):
                pe.matmul(bank[:, 0:D], bcol[:, c % 2, :], f32(wfc[:, HI, c, :]), start=(c == 0), stop=False)
                return pe.matmul(bank[:, 0:D], bcol[:, c % 2, :], f32(wfc[:, LO, c, :]), start=False,
                                 stop=(c == NC_F - 1))
            col_read[c % 2] = token = step("tensor", "bias_mm", fold, [made, weights, taken])
        fcb_ready = step("vector", "bias", lambda v, bank=bank: v.tensor_tensor(
            fcb[:], bank[:, 0:D], fcb[:], ALU.add), [token, consts])
        banks.give(index, fcb_ready)

        wo_t, wga = stage[0][:, 0:KD * D], stage[1][:, 0:KD * D]
        got = [load(f"raw{i}", lambda sp, dst=dst, src=src: sp.dma_start(
            dst.rearrange("p (k n) -> p k n", k=KD), src.rearrange("(k p) n -> p k n", p=P)), [stage_free[i]])
            for i, (dst, src) in enumerate(((wo_t, t["wo_t"]), (wga, t["wg"][0:D, :])))]
        for i in range(KD):
            index, bank, taken = banks.take()

            def wo_wg(pe, i=i, bank=bank):
                for k in range(KD):
                    last = pe.matmul(bank[:, 0:D], wo_t[:, k * D + i * P:k * D + (i + 1) * P],
                                     wga[:, k * D:(k + 1) * D], start=(k == 0), stop=(k == KD - 1))
                return last
            token = step("tensor", "bias_mm", wo_wg, got + [taken])
            done = step("vector", "bias", lambda v, i=i, bank=bank: v.tensor_copy(
                wog[:, i, D:2 * D], bank[:, 0:D]), [token])
            banks.give(index, done)
        index, bank, taken = banks.take()
        for k in range(KD):
            made = step("vector", "bcol_made", lambda v, k=k: v.tensor_scalar(
                bcol[:, k % 2, :], ones[:], bo_col[:, k:k + 1], None, ALU.mult), [col_read[k % 2], consts])
            token = step("tensor", "bias_mm", lambda pe, k=k, bank=bank: pe.matmul(
                bank[:, 0:D], bcol[:, k % 2, :], wga[:, k * D:(k + 1) * D], start=(k == 0), stop=(k == KD - 1)),
                [made, taken] + got)
        ready = step("vector", "bias", lambda v, bank=bank: v.tensor_tensor(
            bog[:, D:2 * D], bank[:, 0:D], bog[:, D:2 * D], ALU.add), [token, consts])
        banks.give(index, ready)
        hid_free, kblock_free = token, token

        setup = step("vector", "bias", lambda v: v.tensor_copy(
            wk1[:].rearrange("p k (j e) -> p k j e", j=HPC),
            wkv1[:, 0, :, :].unsqueeze(2).broadcast_to([P, KD, HPC, HD])), [consts])

        done = {}

        def of(stage, *index):
            return None if index[0] < 0 else done[stage, index]

        scratch_free = [None] * NT
        scratch_at = [0]
        soft_free, softT_free = [None] * NS, [None] * NS

        def layernorm_stats(tag, sources, st, mo, rs, after):
            n = len(sources)
            if True:
                def bn(v):
                    for i, src in enumerate(sources):
                        last = v.bn_stats(st[:, i, :], src)
                    return last
                a = step("vector", f"{tag}_stats", bn, after)

                def aggregate(v):
                    for i in range(n):
                        last = v.bn_aggr(mo[:, i, :], st[:, i, :])
                    return last
                a = step("vector", f"{tag}_stats", aggregate, [a])
                a = step("vector", f"{tag}_stats", lambda v: v.tensor_scalar(
                    rs[:, 0:n], mo[:, 0:n, 1], EPS0, None, ALU.add), [a])
            return step("gpsimd", f"{tag}_rstd", lambda p: p.tensor_tensor(
                rs[:, 0:n], rs[:, 0:n], half_exp[:, 0:n], ALU.pow), [a, filled])

        def normalise(tag, src, mo, rs, i, after):
            slot = scratch_at[0] % NT
            scratch_at[0] += 1
            token = step("vector", f"{tag}_norm", lambda v: v.tensor_scalar(
                normed[:, slot, :], src, mo[:, i, 0:1], rs[:, i:i + 1], ALU.subtract, ALU.mult),
                list(after) + [scratch_free[slot]])
            return slot, token

        def to_feature_major(tag, pieces, after):
            index, bank, taken = banks.take()
            view = bank[:].rearrange("p (k n) -> p k n", k=KD)

            def transposes(pe):
                for b, src in enumerate(pieces):
                    for k in range(KD):
                        last = pe.transpose(view[:, k, b * SEQ:(b + 1) * SEQ], src[:, k * P:(k + 1) * P], ident[:])
                return last
            token = step("tensor", f"{tag}_turned", transposes, list(after) + [taken, selected])
            return index, view, token

        def split_out(tag, bank_view, dst, token, free):
            hi = step("scalar", f"{tag}_hi", lambda a: a.copy(dst(HI), bank_view), [token] + list(free))
            return step("vector", f"{tag}_lo", lambda v: v.tensor_tensor(
                dst(LO), bank_view, f32(dst(HI)), ALU.subtract), [token, hi] + list(free))

        def fetch(g):
            s = g % 2
            done["x", (g,)] = load(f"load_x{s}", lambda sp: sp.dma_start(
                X[:, s, :, :], t["x"][g * GROUP:(g + 1) * GROUP].rearrange("b t d -> t b d")), [of("x1", g - 2)])
            done["c", (g,)] = load("load_c", lambda sp: sp.dma_start(
                C[:], t["ctx"][g * GROUP:(g + 1) * GROUP].rearrange("b t d -> t b d")),
                [of("c_norm", g - 1), of("rawc_turned", g - 1)])

        def front_stats(g):
            s = g % 2
            done["ln", (g,)] = layernorm_stats(
                "ln0", [X[:, s, b, :] for b in range(GROUP)] + [C[:, b, :] for b in range(GROUP)],
                stats, moments, rstd, [of("x", g), of("c", g), of("x_norm", g - 1), of("c_norm", g - 1)])

        def front_norm(g, which):
            name = "xc"[which]
            pieces, tokens = [], []
            for b in range(GROUP):
                src = X[:, g % 2, b, :] if which == 0 else C[:, b, :]
                slot, token = normalise(name, src, moments, rstd, which * GROUP + b, [of("ln", g)])
                pieces.append(slot)
                tokens.append(token)
            done[name + "_norm", (g,)] = tokens[-1]
            state[name, g] = pieces

        def front_turn(g, which):
            name, dst = "xc"[which], (xT, cT)[which]
            pieces = state.pop((name, g))
            index, view, turned = to_feature_major(name, [normed[:, s, :] for s in pieces], [of(name + "_norm", g)])
            for s in pieces:
                scratch_free[s] = turned
            readers = [of("proj_qk", g - 1, NQ - 1)] + ([of("proj_v", g - 1, NQ - 1)] if which else [])
            lo = split_out(name, view, lambda part: dst[:, part, :, :], turned, readers)
            banks.give(index, lo)
            done[name + "T", (g,)] = lo

        def turn_raw(g):
            index, view, turned = to_feature_major("rawc", [C[:, b, :] for b in range(GROUP)], [of("c", g)])
            done["rawc_turned", (g,)] = turned
            done["raw", (g,)] = step("scalar", "rawc_copy", lambda a: a.copy(rawcT[:], view),
                                     [turned, of("proj_kv1", g - 1)])
            banks.give(index, done["raw", (g,)])

        def proj_kv1(g):
            index, bank, taken = banks.take()

            def proj(pe):
                for k in range(KD):
                    pe.matmul(bank[:, 0:TOK], wk1[:, k, :], rawcT[:, k, :], start=(k == 0), stop=(k == KD - 1))
                for b in range(GROUP):
                    for k in range(KD):
                        last = pe.matmul(bank[:, TOK + b * HD:TOK + (b + 1) * HD], rawcT[:, k, b * SEQ:(b + 1) * SEQ],
                                         wkv1[:, 1, k, :], start=(k == 0), stop=(k == KD - 1))
                return last
            mm = done["proj_kv1", (g,)] = step("tensor", "proj_kv1", proj, [of("raw", g), taken, setup, consts])
            step("vector", "k1_out", lambda v: v.tensor_scalar(
                k1T[:, g % NK1, :], bank[:, 0:TOK], bk1[:, 0:1], None, ALU.add),
                [mm, of("kblock", g - NK1, GROUP - 1, 1)])
            done["v1", (g,)] = step("vector", "k1_out", lambda v: v.tensor_tensor(
                v1[:, g % NK1, :, :], bank[:, TOK:TOK + GROUP * HD].rearrange("p (b e) -> p b e", b=GROUP),
                bv1[:].unsqueeze(1).broadcast_to([P, GROUP, HD]), ALU.add), [of("vpad", g - NK1, GROUP - 1)])
            banks.give(index, done["v1", (g,)])

        def proj_qk(g, Q):
            s = Q % 2
            for w, src, dst, bias, name in ((wq, xT, qT, bq, "q"), (wk, cT, kT, bk, "k")):
                index, bank, taken = banks.take()

                def mms(pe, w=w, src=src, bank=bank):
                    for c in range(QC):
                        cols = slice((Q * QC + c) * P, (Q * QC + c + 1) * P)
                        for k in range(KD):
                            last = mm3(pe, bank[:, c * TOK:(c + 1) * TOK], lambda part: w[:, part, k, cols],
                                       lambda part: src[:, part, k, :], k == 0, k == KD - 1)
                    return last
                mm = step("tensor", "proj_qk", mms, [of("xT", g), of("cT", g), taken, weights])
                free = of("scores", *(prev_unit(g, Q)))

                if name == "q":
                    def out(a, bank=bank):
                        for c in range(QC):
                            i = Q * QC + c
                            last = a.activation(qT[:, s, c, :], bank[:, c * TOK:(c + 1) * TOK], ACT.Identity,
                                                bias=bq[:, i:i + 1])
                        return last
                    token = step("scalar", "q_out", out, [mm, free, bias_done["q"]])
                else:
                    def out(v, bank=bank):
                        for c in range(QC):
                            i = Q * QC + c
                            last = v.tensor_scalar(kT[:, s, c, :], bank[:, c * TOK:(c + 1) * TOK], bk[:, i:i + 1],
                                                   None, ALU.add)
                        return last
                    token = step("vector", "k_out", out, [mm, free])
                banks.give(index, token)
                done[name, (g, Q)] = token
            done["proj_qk", (g, Q)] = mm

        def prev_unit(g, Q):
            n = g * NQ + Q - 2
            return (n // NQ, (n % NQ) * GROUP + GROUP - 1)

        def proj_v(g, Q):
            s = Q % 2
            index, bank, taken = banks.take()

            def mms(pe):
                for b in range(GROUP):
                    for k in range(KD):
                        last = mm3(pe, bank[:, b * QW:(b + 1) * QW], lambda part: cT[:, part, k, b * SEQ:(b + 1) * SEQ],
                                   lambda part: wv[:, part, k, Q * QW:(Q + 1) * QW], k == 0, k == KD - 1)
                return last
            mm = done["proj_v", (g, Q)] = step("tensor", "proj_v", mms, [of("cT", g), taken, weights])
            token = done["v", (g, Q)] = step("vector", "v_out", lambda v: v.tensor_copy(
                V[:, s, :, :].rearrange("p b n -> p (b n)"), bank[:]), [mm, of("pv", *prev_unit(g, Q))])
            banks.give(index, token)

        def biased_max(index, bank, bias_tile, scale, scored, slot):
            def add_max(v):
                for h in range(QUAD):
                    last = v.tensor_tensor_reduce(soft[:, slot, h, :], bank[:, h * SEQ:(h + 1) * SEQ], bias_tile[:],
                                                  1.0, LOWEST, ALU.add, ALU.max, row_max[:, slot, h:h + 1])
                return last
            m = step("vector", "score_max", add_max, [scored, soft_free[slot], consts, masks])
            banks.give(index, m)
            return step("vector", "score_max", lambda v: v.tensor_scalar(
                neg_max[:, slot, :], row_max[:, slot, :], -scale, None, ALU.mult), [m])

        def exponentials(key):
            slot, scale, m = state[key]

            def exps(a):
                for h in range(QUAD):
                    last = a.activation(soft[:, slot, h, :], soft[:, slot, h, :], ACT.Exp,
                                        bias=neg_max[:, slot, h:h + 1], scale=scale,
                                        accum_out=row_sum[:, slot, h:h + 1])
                return last
            state[key] = (slot, step("scalar", "exps", exps, [m]))

        def divide(key):
            slot, e = state[key]
            r = step("vector", "sum_inv", lambda v: v.reciprocal(inv_sum[:, slot, :], row_sum[:, slot, :]), [e])
            state[key] = (slot, step("gpsimd", "norm_" + key[0], lambda p: p.tensor_tensor(
                soft[:, slot, :, :], soft[:, slot, :, :],
                inv_sum[:, slot, :].unsqueeze(2).broadcast_to([P, QUAD, SEQ]), ALU.mult), [e, r]))

        def turn_probs(block, slot, normed_token, on_scalar):
            index, bank, taken = banks.take()

            def transposes(pe):
                for h in range(QUAD):
                    last = pe.transpose(bank[:, h * SEQ:(h + 1) * SEQ], soft[:, slot, h, :], ident[:])
                return last
            turned = step("tensor", f"probs{block}_turned", transposes, [normed_token, taken])
            soft_free[slot] = turned
            dst = softT[:, slot, :, :].rearrange("p h n -> p (h n)")
            if on_scalar:
                token = step("scalar", "probs_out_s", lambda a: a.copy(dst, bank[:]), [turned, softT_free[slot]])
            else:
                token = step("vector", "probs_out_v", lambda v: v.tensor_copy(dst, bank[:]), [turned, softT_free[slot]])
            banks.give(index, token)
            return token

        state = {}

        def tiles(m):
            return m // 2, m % 2 * HS, [(c, b) for c in range(QC) for b in range(GROUP)]

        def scores(g, m):
            Q, r, which = tiles(m)
            s = Q % 2
            index, bank, taken = banks.take()

            def mms(pe):
                for h, (c, b) in enumerate(which):
                    last = pe.matmul(bank[:, h * SEQ:(h + 1) * SEQ], qT[r:r + HS, s, c, b * SEQ:(b + 1) * SEQ],
                                     kT[r:r + HS, s, c, b * SEQ:(b + 1) * SEQ], start=True, stop=True)
                return last
            mm = done["scores", (g, m)] = step("tensor", "scores", mms, [of("q", g, Q), of("k", g, Q), taken])
            slot = m % 2
            state["a0", g, m] = (slot, SCALE0, biased_max(index, bank, relb, SCALE0, mm, slot))

        def turn0(g, m):
            slot, token = state["a0", g, m]
            state["a0", g, m] = (slot, turn_probs(0, slot, token, m % 2 == 0))

        def pv0(g, m):
            Q, r, which = tiles(m)
            s = Q % 2
            slot, token = state.pop(("a0", g, m))
            if r == 0:
                state["o0"] = banks.take()
            index, bank, taken = state["o0"]

            def mms(pe):
                for h, (c, b) in enumerate(which):
                    col = (b * QC + c) * SEQ
                    last = pe.matmul(bank[r:r + HS, col:col + SEQ], V[:, s, b, c * P + r:c * P + r + HS],
                                     softT[:, slot, h, :], start=True, stop=True)
                return last
            mm = done["pv", (g, m)] = step("tensor", "pv", mms, [token, of("v", g, Q), taken])
            softT_free[slot] = mm
            if r:
                dst = lambda part: OT[:, part, :, :, :].rearrange("p b c n -> p (b c n)")
                lo = split_out("o", bank[:], dst, mm, [state.get("fc_read")])
                banks.give(index, lo)
                state["oT"] = lo

        def fc(g, Q):
            if Q == 0:
                state["fc"] = banks.take()
            index, bank, taken = state["fc"]
            token = state["oT"]

            def mms(pe):
                for b in range(GROUP):
                    for c in range(QC):
                        last = mm3(pe, bank[:, b * D:(b + 1) * D], lambda part: OT[:, part, b, c, :],
                                   lambda part: wfc[:, part, Q * QC + c, :], Q == 0 and b == 0 and c == 0,
                                   Q == NQ - 1 and c == QC - 1, skip_group_check=True)
                return last
            state["fc_read"] = step("tensor", "fc", mms, [token, taken, weights])

        def finish_attention(g):
            s = g % 2
            xs = x1[:, s, :, :]
            index, bank, _ = state["fc"]
            xb = step("gpsimd", "x_plus_fcb", lambda p: p.tensor_tensor(
                X[:, s, :, :], X[:, s, :, :], fcb[:].unsqueeze(1).broadcast_to([P, GROUP, D]), ALU.add),
                [of("x", g), of("x_norm", g), fcb_ready])
            x1_done = done["x1", (g,)] = step("vector", "x1", lambda v: v.tensor_tensor(
                xs.rearrange("p b d -> p (b d)"), bank[:], X[:, s, :, :].rearrange("p b d -> p (b d)"), ALU.add),
                [state["fc_read"], xb, of("x1_read", g - 2)])
            banks.give(index, x1_done)
            rs = layernorm_stats("ln2", [xs[:, b, :] for b in range(GROUP)], stats2, moments2, rstd2, [x1_done])
            pieces, tokens = [], []
            for b in range(GROUP):
                slot, token = normalise("h", xs[:, b, :], moments2, rstd2, b, [rs])
                pieces.append(slot)
                tokens.append(token)
            done["x1b", (g,)] = step("gpsimd", "x1_plus_b2", lambda p: p.tensor_tensor(
                xs, xs, b2[:].unsqueeze(1).broadcast_to([P, GROUP, D]), ALU.add), [tokens[-1], consts])
            state["h", g] = (pieces, tokens)

        def turn_h(g):
            pieces, tokens = state.pop(("h", g))
            index, view, turned = to_feature_major("h", [normed[:, s, :] for s in pieces], tokens)
            for s in pieces:
                scratch_free[s] = turned
            lo = split_out("h", view, lambda part: hT[:, part, :, :], turned, [of("w1", g - 1, 1)])
            banks.give(index, lo)
            done["hT", (g,)] = lo

        def mlp_in(g, half, pair):
            index, bank, taken = banks.take()
            first = half * HH + pair * 2

            def mms(pe):
                for c in range(2):
                    for k in range(KD):
                        last = mm3(pe, bank[:, c * TOK:(c + 1) * TOK],
                                   lambda part: w1[:, part, k, (first + c) * P:(first + c + 1) * P],
                                   lambda part: hT[:, part, k, :], k == 0, k == KD - 1)
                return last
            mm = done["w1", (g, half)] = step("tensor", "w1", mms, [of("hT", g), taken, weights])

            def out(a):
                for c in range(2):
                    last = a.activation(hid[:, pair * 2 + c, :], bank[:, c * TOK:(c + 1) * TOK], ACT.Identity,
                                        bias=b1[:, first + c:first + c + 1])
                return last
            token = step("scalar", "hid_out", out, [mm, state.get("hid_read", hid_free), bias_done["1"]])
            banks.give(index, token)
            state["hid"] = token

        def gelu(g, half):
            flat = hid[:].rearrange("p c n -> p (c n)")
            act = step("scalar", "gelu", lambda a: a.activation(flat, flat, ACT.Gelu), [state["hid"]])
            hi = step("vector", "hid_hi", lambda v: v.tensor_copy(
                hidS[:, HI, :, :].rearrange("p c n -> p (c n)"), flat), [act, state.get("w2_read")])
            lo = step("vector", "hid_lo", lambda v: v.tensor_tensor(
                hidS[:, LO, :, :].rearrange("p c n -> p (c n)"), flat,
                f32(hidS[:, HI, :, :]).rearrange("p c n -> p (c n)"), ALU.subtract), [hi, act])
            state["hid_read"] = lo
            state["hidS"] = lo

        def mlp_out(g, half, b):
            if half == 0 and b == 0:
                state["w2"] = banks.take()
            index, bank, taken = state["w2"]

            def mms(pe):
                for c in range(HH):
                    last = mm3(pe, bank[:, b * D:(b + 1) * D], lambda part: hidS[:, part, c, b * SEQ:(b + 1) * SEQ],
                               lambda part: w2[:, part, half * HH + c, :], half == 0 and b == 0 and c == 0,
                               half == 1 and c == HH - 1, skip_group_check=True)
                return last
            state["w2_read"] = step("tensor", "w2", mms, [state["hidS"], taken, weights])

        def block1_in(g):
            index, bank, _ = state["w2"]
            flat = x1[:, g % 2, :, :].rearrange("p b d -> p (b d)")
            x2 = done["x2", (g,)] = step("vector", "x2", lambda v: v.tensor_tensor(flat, bank[:], flat, ALU.add),
                                         [state["w2_read"], of("x1b", g)])
            banks.give(index, x2)

        def turn_x2(g):
            index, view, turned = to_feature_major("x2", [x1[:, g % 2, b, :] for b in range(GROUP)], [of("x2", g)])
            token = done["x2T", (g,)] = step("scalar", "x2_out", lambda a: a.copy(x2T[:], view),
                                             [turned, of("out_mm", g - 1, GROUP - 1)])
            banks.give(index, token)

        def proj_q1(g):
            index, bank, taken = banks.take()

            def mms(pe):
                for c in range(KD):
                    for k in range(KD):
                        last = pe.matmul(bank[:, c * TOK:(c + 1) * TOK], wq1[:, k, c * P:(c + 1) * P], x2T[:, k, :],
                                         start=(k == 0), stop=(k == KD - 1))
                return last
            mm = step("tensor", "proj_q1", mms, [of("x2T", g), taken, consts])

            def out(a):
                for c in range(KD):
                    last = a.activation(q1T[:, c, :], bank[:, c * TOK:(c + 1) * TOK], ACT.Identity,
                                        bias=bq1[:, c:c + 1])
                return last
            token = done["q1", (g,)] = step("scalar", "q1_out", out, [mm, of("scores1", g - 1, GROUP - 1, NU1 - 1)])
            banks.give(index, token)

        def before(g, b):
            return (g, b - 1) if b else (g - 1, GROUP - 1)

        def spread_k(g, b, half):
            heads = slice(half * QUAD, (half + 1) * QUAD)
            done["kblock", (g, b, half)] = step("gpsimd", "kblock", lambda p: p.tensor_tensor(
                kblock[:, heads, :], k1T[:, g % NK1, b * SEQ:(b + 1) * SEQ].unsqueeze(1).broadcast_to([P, QUAD, SEQ]),
                block_of[:, heads].unsqueeze(2).broadcast_to([P, QUAD, SEQ]), ALU.mult),
                [of("v1", g), of("scores1", *before(g, b), NU1 - 2 + half) or kblock_free, masks])

        def spread_v(g, b):
            done["vpad", (g, b)] = step("gpsimd", "vpad", lambda p: p.tensor_copy(
                vpad[:].rearrange("p (j n) -> p j n", n=VSTEP)[:, :, 0:HD],
                v1[:, g % NK1, b, :].unsqueeze(1).broadcast_to([P, HPC, HD])),
                [of("v1", g), of("pv1", *before(g, b), NU1 - 1), filled])

        def scores1(g, b, u):
            index, bank, taken = banks.take()
            c, j = u * QUAD // HPC, u * QUAD % HPC
            mm = done["scores1", (g, b, u)] = step("tensor", "scores1", lambda pe: pe.matmul(
                bank[:], q1T[:, c, b * SEQ:(b + 1) * SEQ], kblock[:, j:j + QUAD, :], start=True, stop=True),
                [of("q1", g), of("kblock", g, b, j // QUAD), taken])
            slot = 2 + u % 2
            state["a1", g, b, u] = (slot, SCALE1, biased_max(index, bank, winb, SCALE1, mm, slot))

        def turn1(g, b, u):
            slot, token = state["a1", g, b, u]
            state["a1", g, b, u] = (slot, turn_probs(1, slot, token, u % 2 == 1))

        def pv1(g, b, u):
            slot, token = state.pop(("a1", g, b, u))
            if u == 0:
                state["o1"] = banks.take()
            index, bank, taken = state["o1"]
            c, j = u * QUAD // HPC, u * QUAD % HPC

            def mms(pe):
                for h in range(QUAD):
                    last = pe.matmul(bank[:, c * SEQ:(c + 1) * SEQ], vpad[:, (j + h) * P:(j + h + 1) * P],
                                     softT[:, slot, h, :], start=(j + h == 0), stop=(j + h == HPC - 1))
                return last
            mm = done["pv1", (g, b, u)] = step("tensor", "pv1", mms, [token, of("vpad", g, b), taken])
            softT_free[slot] = mm
            if u == NU1 - 1:
                pg, pb = before(g, b)
                token = done["o1", (g, b)] = step("vector", "o1_out", lambda v: v.tensor_copy(
                    o1T[:].rearrange("p c n -> p (c n)"), bank[:, 0:KD * SEQ]), [mm, of("out_mm", pg, pb)])
                banks.give(index, token)

        def out_mm(g, b):
            index, bank, taken = banks.take()

            def mms(pe):
                pe.matmul(bank[:], o1T[:, 0, :], wog[:, 0, :], start=True, stop=False)
                for k in range(KD):
                    pe.matmul(bank[:, D:2 * D], x2T[:, k, b * SEQ:(b + 1) * SEQ], wgx[:, k, :],
                              start=False, stop=False, skip_group_check=True)
                return pe.matmul(bank[:], o1T[:, 1, :], wog[:, 1, :], start=False, stop=True)
            mm = done["out_mm", (g, b)] = step("tensor", "out_mm", mms, [of("o1", g, b), of("x2T", g), taken, setup])
            pg, pb = before(g, b)
            a0 = step("vector", "ag", lambda v: v.tensor_tensor(ag[:], bank[:], bog[:], ALU.add),
                      [mm, of("mix1", pg, pb), ready])
            banks.give(index, a0)
            th = step("scalar", "tanh", lambda a: a.activation(gate[:], ag[:, D:2 * D], ACT.Tanh, scale=0.5),
                      [a0, of("mix1", pg, pb)])
            df = step("gpsimd", "mix", lambda p: p.tensor_tensor(ag[:, 0:D], ag[:, 0:D], x1[:, g % 2, b, :], ALU.subtract),
                      [a0, of("mix2", pg, pb)])
            g1 = step("vector", "gate", lambda v: v.tensor_scalar(gate[:], gate[:], 0.5, 0.5, ALU.mult, ALU.add), [th])
            g2 = step("gpsimd", "mix", lambda p: p.tensor_tensor(gate[:], gate[:], ag[:, D:2 * D], ALU.mult), [g1])
            m1 = done["mix1", (g, b)] = step("gpsimd", "mix", lambda p: p.tensor_tensor(
                ag[:, 0:D], ag[:, 0:D], gate[:], ALU.mult), [g2, df])
            m2 = done["mix2", (g, b)] = step("gpsimd", "mix", lambda p: p.tensor_tensor(
                mixed[:], ag[:, 0:D], x1[:, g % 2, b, :], ALU.add), [m1, of("mix_read", pg, pb)])
            if b == GROUP - 1:
                done["x1_read", (g,)] = m2
            sq = step("scalar", "square", lambda a: a.activation(gate[:], mixed[:], ACT.Square,
                                                                 accum_out=sumsq[:, 0:1]), [m2])
            done["mix1", (g, b)] = sq
            ms = step("vector", "gate", lambda v: v.tensor_scalar(
                rrms[:], sumsq[:], 1.0 / D, EPS1, ALU.mult, ALU.add), [sq, of("mix_read", pg, pb)])
            rr = step("gpsimd", "rrms", lambda p: p.tensor_tensor(rrms[:], rrms[:], half_exp[:, 0:1], ALU.pow), [ms])
            pc = of("center", pg, pb)
            xh = step("vector", "x_hat", lambda v: v.scalar_tensor_tensor(
                mixed[:], mixed[:], rrms[:, 0:1], rmsw[:], ALU.mult, ALU.mult), [rr, sq, m2, pc])
            state["xhat", g, b] = xh

        def center_out(g, b):
            xh = state.pop(("xhat", g, b))
            index, bank, taken = banks.take()
            mm = done["center", (g, b)] = step("tensor", "center", lambda pe: pe.matmul(
                bank[:, 0:D], center[:], mixed[:], start=True, stop=True), [xh, taken, selected])
            done["mix_read", (g, b)] = mm
            n = g * GROUP + b
            y = step("scalar", "y_out", lambda a: a.copy(Y[:], bank[:, 0:D]), [mm, of("stored", n - 1)])
            banks.give(index, y)
            done["stored", (n,)] = load("store", lambda sp: sp.dma_start(t["out"][n], Y[:]), [y])

        UNITS = NQ * 2

        def on(engine, work, tokens=lambda: []):
            return engine, tokens, work

        def pe(work, tokens=lambda: []):
            return on("tensor", work, lambda: list(tokens()) + [banks.next_token()])

        def softmax_pieces(key):
            return (on("scalar", lambda: exponentials(key), lambda: [state[key][2]]),
                    on("vector", lambda: divide(key), lambda: [state[key][1]]))

        def mlp_stream(g):
            into = lambda half, pair: pe(lambda: mlp_in(g, half, pair), lambda: [of("hT", g), state.get("hid_read")])
            act = lambda half: on("scalar", lambda: gelu(g, half), lambda: [state["hid"]])
            out = lambda half, b: pe(lambda: mlp_out(g, half, b), lambda: [state["hidS"]])
            return [pe(lambda: turn_h(g), lambda: state["h", g][1]),
                    into(0, 0), into(0, 1), act(0), into(1, 0), out(0, 0), out(0, 1), into(1, 1), act(1),
                    out(1, 0), out(1, 1), on("vector", lambda: block1_in(g), lambda: [state["w2_read"]]),
                    on("sync", lambda: block1_queue.extend(block1_stream(g)))]

        def block1_stream(g):
            pieces = [on("gpsimd", lambda: (spread_k(g, 0, 0), spread_k(g, 0, 1), spread_v(g, 0))),
                      pe(lambda: turn_x2(g), lambda: [of("x2", g)]), pe(lambda: proj_q1(g), lambda: [of("x2T", g)])]
            units = [(b, u) for b in range(GROUP) for u in range(NU1)]
            soften = [softmax_pieces(("a1", g) + unit) for unit in units]
            for n in range(len(units) + 3):
                if n < len(units):
                    b, u = units[n]
                    pieces.append(pe(lambda b=b, u=u: scores1(g, b, u),
                                     lambda b=b, u=u: [of("q1", g), of("kblock", g, b, u % 2)]))
                    if u >= NU1 - 2 and b + 1 < GROUP:
                        pieces.append(on("gpsimd", lambda b=b, u=u: spread_k(g, b + 1, u - NU1 + 2)))
                if 2 <= n and n - 2 < len(units):
                    b, u = units[n - 2]
                    pieces.append(pe(lambda b=b, u=u: pv1(g, b, u), lambda b=b, u=u: [state["a1", g, b, u][1]]))
                    if u == NU1 - 1 and b + 1 < GROUP:
                        pieces.append(on("gpsimd", lambda b=b: spread_v(g, b + 1)))
                if n < len(units):
                    pieces.append(soften[n][0])
                if 1 <= n and n - 1 < len(units):
                    b, u = units[n - 1]
                    pieces.append(pe(lambda b=b, u=u: turn1(g, b, u), lambda b=b, u=u: [state["a1", g, b, u][1]]))
                if n < len(units):
                    pieces.append(soften[n][1])
                if 3 <= n and units[n - 3][1] == NU1 - 1:
                    b = units[n - 3][0]
                    pieces.append(pe(lambda b=b: (center_due(), out_mm(g, b), later.append((g, b))),
                                     lambda b=b: [of("o1", g, b)]))
            return pieces

        mlp_queue, block1_queue = [], []
        later = []

        def center_due():
            while later:
                center_out(*later.pop(0))

        def finish_group(g):
            while g >= 2 and ("x1_read", (g - 2,)) not in done:
                (block1_queue if block1_queue else mlp_queue).pop(0)[2]()
            finish_attention(g)

        def attention_pieces(n):
            g, m = n // UNITS, n % UNITS
            unit = lambda n: (n // UNITS, n % UNITS)
            running = n < NG * UNITS
            pieces = []
            if running:
                soften = softmax_pieces(("a0", g, m))
                pieces.append(pe(lambda: scores(g, m), lambda: [of("q", g, m // 2), of("k", g, m // 2)]))
            k = n - 3
            if k >= 0 and k % 2 == 1 and k < NG * UNITS:
                kg, kq = k // UNITS, (k % UNITS) // 2
                pieces.append(pe(lambda: fc(kg, kq), lambda: [state["oT"]]))
                if kq == NQ - 1:
                    pieces.append(on("vector", lambda: finish_group(kg)))
            if running and m == 1:
                pieces.append(pe(lambda: turn_raw(g), lambda: [of("c", g)]))
            if running and m == 2:
                pieces.append(pe(lambda: proj_kv1(g), lambda: [of("raw", g)]))
            if running:
                pieces.append(soften[0])
            if g + 1 < NG:
                if m == 3:
                    pieces.append(on("sync", lambda: fetch(g + 1)))
                if m == 4:
                    pieces.append(on("vector", lambda: front_stats(g + 1)))
                if m == 5:
                    pieces.append(on("vector", lambda: (front_norm(g + 1, 0), front_norm(g + 1, 1))))
                if m == UNITS - 2:
                    pieces += [pe(lambda: front_turn(g + 1, 0), lambda: [of("x_norm", g + 1)]),
                               pe(lambda: front_turn(g + 1, 1), lambda: [of("c_norm", g + 1)])]
            gq, q = (g, m // 2 + 1) if m // 2 + 1 < NQ else (g + 1, 0)
            if gq < NG and (m % 2 == 0 if gq == g else m == UNITS - 1):
                pieces.append(pe(lambda: proj_qk(gq, q), lambda: [of("xT", gq), of("cT", gq)]))
            if 2 <= n and n - 2 < NG * UNITS:
                pieces.append(pe(lambda: pv0(*unit(n - 2)), lambda: [state[("a0",) + unit(n - 2)][1]]))
            if gq < NG and m % 2 == 1:
                pieces.append(pe(lambda: proj_v(gq, q), lambda: [of("cT", gq)]))
            if running:
                pieces.append(soften[1])
            if 1 <= n and n - 1 < NG * UNITS:
                pieces.append(pe(lambda: turn0(*unit(n - 1)), lambda: [state[("a0",) + unit(n - 1)][1]]))
            if n >= UNITS + 3 and (n - 3) % UNITS == 0:
                pieces.append(on("sync", lambda: mlp_queue.extend(mlp_stream(n // UNITS - 1))))
            return pieces

        fetch(0)
        front_stats(0)
        front_norm(0, 0)
        front_norm(0, 1)
        front_turn(0, 0)
        front_turn(0, 1)
        proj_qk(0, 0)
        proj_v(0, 0)
        MLP_RATE, BLOCK1_RATE, CENTER_RATE, LAG_PER_STALL = 2.2, 7.5, 0.5, 0.3
        step_now, attention_queue, at, size = 0, attention_pieces(0), 0.0, 1
        place = {"mlp": 0.0, "block1": 0.0, "center": 0.0}
        while True:
            if not attention_queue and step_now + 1 < NG * UNITS + 4:
                step_now += 1
                attention_queue = attention_pieces(step_now)
                size = max(len(attention_queue), 1)
            if attention_queue:
                at = step_now + 1 - len(attention_queue) / size
            heads = []
            if attention_queue:
                heads.append((at, attention_queue[0], attention_queue, None, 0))
            for name, queue, rate in (("mlp", mlp_queue, MLP_RATE), ("block1", block1_queue, BLOCK1_RATE)):
                if queue:
                    heads.append((place[name], queue[0], queue, name, 1.0 / rate))
                else:
                    place[name] = at
            if later:
                g, b = later[0]
                heads.append((place["center"] + 1, pe(center_due, lambda: [state["xhat", g, b]]), None, "center", 0))
            else:
                place["center"] = at
            if not heads:
                break

            def cost(head):
                engine, tokens, _ = head[1]
                return head[0] + LAG_PER_STALL * max(0.0, S.reached(tokens()) - S.clock[engine])
            _, piece, queue, name, pace = min(heads, key=cost)
            if queue is not None:
                queue.pop(0)
            if name:
                place[name] += pace
            piece[2]()
        name, value = done["stored", (NBATCH - 1,)]
        fin = [(S.sem[name], value)]

        block = ctx.enter_context(nc.Block())

        @block.sync
        def _(eng):
            S.replay("sync", eng)
            for sem, value in fin:
                eng.wait_ge(sem, value)

        @block.tensor
        def _(eng):
            S.replay("tensor", eng)

        @block.vector
        def _(eng):
            S.replay("vector", eng)

        @block.scalar
        def _(eng):
            S.replay("scalar", eng)

        @block.gpsimd
        def _(eng):
            S.replay("gpsimd", eng)


def kernel(x, ctx_1024, **w):
    import concourse.bacc as bacc
    from concourse.bass_utils import run_bass_kernel_spmd

    D = x.shape[2]
    T = x.shape[1]
    a = {k.replace("L0_xattn_", "0").replace("L1_xattn_", "1"): v for k, v in w.items()}
    rel = a["0rel_bias"]
    ntok = (rel.shape[0] + 1) // 2


    def columns(v):
        return v.reshape(-1, P).T

    arrays = {
        "x": x, "ctx": ctx_1024,
        "wq_t": a["0Wq"].reshape(-1, D).T, "wk_t": a["0Wk"].reshape(-1, D).T, "wv_t": a["0Wv"].reshape(-1, D).T,
        "fc_t": a["0fc_w"].T, "w1_t": a["0W1"].T, "w2_t": a["0W2"].T,
        "ln_q_g": columns(a["0ln_q_g"]), "ln_q_b": columns(a["0ln_q_b"]), "ln_k_g": columns(a["0ln_k_g"]), "ln_k_b": columns(a["0ln_k_b"]),
        "ln_v_g": columns(a["0ln_v_g"]), "ln_v_b": columns(a["0ln_v_b"]), "ln2_g": columns(a["0ln2_g"]), "ln2_b": columns(a["0ln2_b"]),
        "fc_b": a["0fc_b"], "b1": columns(a["0b1"]), "b2": a["0b2"],
        "rel": np.stack([rel[r + ntok - T:r + ntok][::-1] for r in range(T)]),
        "wq1": a["1Wq"], "wk1": a["1Wk"], "wv1": a["1Wv"], "bq1": columns(a["1bq"]), "bk1": a["1bk"], "bv1": a["1bv"],
        "wo": a["1Wo"], "wo_t": a["1Wo"].T, "bo": a["1bo"], "bo_col": columns(a["1bo"]), "wg": a["1Wg"], "bg": a["1bg"], "rms_w": a["1rms_w"],
    }
    nc = bacc.Bacc("TRN2", target_bir_lowering=False, num_devices=1)
    ins, tensors = {}, {}
    for name, v in arrays.items():
        v = np.ascontiguousarray(v)
        ins[f"in_{name}"] = v
        tensors[name] = nc.dram_tensor(f"in_{name}", v.shape, mybir.dt.from_np(v.dtype), kind="ExternalInput").ap()
    tensors["out"] = nc.dram_tensor("out_0", x.shape, F32, kind="ExternalOutput").ap()
    two_block_xattn(nc, tensors)
    r = run_bass_kernel_spmd(nc, [ins], core_ids=[0])
    return r.results[0]["out_0"]
```

```python
from contextlib import ExitStack

import numpy as np

from concourse import mybir

F32 = mybir.dt.float32
F32R = mybir.dt.float32r
ALU = mybir.AluOpType
ACT = mybir.ActivationFunctionType

P = 128
HI, LO = 0, 1
BANKS, BANK = 8, 512


class Bank:

    tile, giver = None, None

    def __getitem__(self, key):
        return self.tile[key]

    def give(self, token):
        self.giver = token


class Step:

    def __init__(self, engine, name, value, by, work, after, place):
        self.engine, self.name, self.value, self.by, self.work = engine, name, value, by, work
        self.after, self.place = after, place


class Steps:

    ENGINES = ("sync", "tensor", "vector", "scalar", "gpsimd")
    TABLE = {"gelu": "gelu", "exps0": "exp", "exps1": "exp", "tanh": "exp"}
    LENGTH = dict(
        x_turned=0.43, c_turned=0.43, rawc_turned=0.43, h_turned=0.43, x2_turned=0.43, probs0_turned=0.43,
        probs1_turned=0.43, proj_qk=1.31, proj_v=1.31, proj_kv1=1.2, proj_q1=1.3, scores=1.0, scores1=0.45,
        pv=1.0, pv1=1.0, fc=1.35, w1=1.35, w2=1.45, out_mm=1.95, center=0.43, bias_mm=3.3, folded=0.85, wo_wg=0.85,
        score_max0=0.85, score_max1=0.85, neg_max0=0.08, neg_max1=0.08, sum_inv0=0.1, sum_inv1=0.1, k_out=0.8,
        v_out=0.6, probs0_out_v=0.6, probs1_out_v=0.6, o_lo=0.6, x_lo=0.6, c_lo=0.6, h_lo=0.6, x2_lo=0.6,
        hid_hi=0.6, hid_lo=1.15, o1_lo=0.33, q1_lo=1.6, k1_out=0.25, kblock_lo=1.05, ag=0.6, gate=0.15, x_hat=0.4,
        x1=0.6, x2=0.6, ln0_stats=0.6, ln2_stats=0.3, x_norm=0.33, c_norm=0.33, h_norm=0.33, bcol_made=0.2,
        bias=0.1, w_lo=1.2,
        exps0=1.7, exps1=1.7, gelu=2.25, tanh=0.31, square=0.4, q_out=0.72, probs0_out_s=0.48, probs1_out_s=0.48,
        o_hi=0.48, x_hi=0.48, c_hi=0.48, h_hi=0.48, x2_hi=0.48, o1_hi=0.26, q1_out=1.43, hid_out=0.72,
        rawc_copy=0.48, y_out=0.26, w_hi=1.0,
        norm_a0=1.0, norm_a1=1.0, kblock=1.0, vpad=0.33, mix=0.69, rrms=0.46, ln0_rstd=0.96, ln2_rstd=0.63,
        x_plus_fcb=1.23, x1_plus_b2=1.23, filled=1.6, selected=1.0,
        raw0=5.0, raw1=5.0, raw2=5.0, raw3=5.0, raw4=5.0, consts=14.0, cols_in=2.2, load_x0=2.5, load_x1=2.5,
        load_c=2.5, store=2.5)
    TABLE_LOAD = 1.3
    HANDOVER = 0.15
    PATIENCE = 0.0
    ISSUE = 0.1

    def __init__(self, nc, ctx, tiles):
        self.nc, self.ctx, self.tiles = nc, ctx, tiles
        self.sem, self.count, self.engine_of = {}, {}, {}
        self.steps = []
        self.queue = {e: [] for e in self.ENGINES}
        self.place = 0.0

    def step(self, engine, name, work, after=(), by=1):
        if name not in self.sem:
            self.sem[name] = self.ctx.enter_context(self.nc.semaphore(name))
            self.count[name], self.engine_of[name] = 0, engine
        assert self.engine_of[name] == engine
        self.count[name] += by
        after = [token for token in after if token is not None]
        self.steps.append(Step(engine, name, self.count[name], by, work, after, self.place))
        return name, self.count[name]

    def order(self):
        ends, clock, table = {}, dict.fromkeys(self.ENGINES, 0.0), None
        lines = {e: {} for e in self.ENGINES}
        for s in self.steps:
            lines[s.engine].setdefault(s.name, []).append(s)
        for e in self.ENGINES:
            for name in lines[e]:
                lines[e][name].reverse()
        freed_by = {token.giver: token for s in self.steps for token in s.after if isinstance(token, Bank)}
        free = [(0.0, i, None) for i in range(len(self.tiles))]

        def ready(s):
            at = 0.0
            for token in s.after:
                if isinstance(token, Bank):
                    if token.tile is None:
                        if not free:
                            return None
                        at = max(at, min(free)[0])
                elif token in ends:
                    at = max(at, ends[token] + self.HANDOVER)
                else:
                    return None
            return at

        left = len(self.steps)
        while left:
            pick = None
            for e in self.ENGINES:
                heads = [(ready(line[-1]), line[-1]) for line in lines[e].values() if line]
                heads = [(at, s) for at, s in heads if at is not None]
                if not heads:
                    continue
                start = max(clock[e], min(at for at, _ in heads))
                at, s = min(((at, s) for at, s in heads if at <= start + self.PATIENCE), key=lambda h: h[1].place)
                if pick is None or start < pick[0]:
                    pick = start, max(start, at), s
            _, start, s = pick
            lines[s.engine][s.name].pop()
            left -= 1
            length = self.LENGTH.get(s.name, 1.0)
            if self.TABLE.get(s.name, table) != table:
                table = self.TABLE[s.name]
                length += self.TABLE_LOAD
            token = (s.name, s.value)
            ends[token] = start + length
            clock[s.engine] = start + (self.ISSUE if s.engine == "sync" else length)
            waits = []
            for t in s.after:
                if not isinstance(t, Bank):
                    waits.append(t)
                elif t.tile is None:
                    free.sort(key=lambda f: f[0])
                    _, t.index, last_reader = free.pop(0)
                    t.tile = self.tiles[t.index]
                    if last_reader is not None:
                        waits.append(last_reader)
            if token in freed_by:
                free.append((ends[token] + self.HANDOVER, freed_by[token].index, token))
            self.queue[s.engine].append((s, waits))

    def load(self, name, work, after=()):
        return self.step("sync", name, work, after, by=16)

    def replay(self, engine, eng):
        passed = {}
        for s, waits in self.queue[engine]:
            for name, value in waits:
                if passed.get(name, 0) < value:
                    passed[name] = value
                    eng.wait_ge(self.sem[name], value)
            s.work(eng).then_inc(self.sem[s.name], s.by)


def two_block_xattn(nc, t):
    NBATCH, SEQ, D = t["x"].shape
    GROUP = 2
    NG = NBATCH // GROUP
    KD = D // P
    TOK = GROUP * SEQ
    F = t["wq_t"].shape[1]
    H0 = 16
    HS = F // H0
    NC_F = F // P
    QUAD = BANK // SEQ
    NQ = H0 // QUAD
    QC = QUAD * HS // P
    QW = QUAD * HS
    H1 = 16
    HD = D // H1
    HPC = P // HD
    NU1 = H1 // QUAD
    WINDOW_HALF = 64
    EPS0, EPS1 = 1e-5, 1e-6
    SCALE0, SCALE1 = float(HS) ** -0.5, float(HD) ** -0.5
    MASKED = -1e30
    LOWEST = -3.0e38
    assert SEQ == P and D == 256

    with ExitStack() as ctx:
        S = Steps(nc, ctx, [ctx.enter_context(nc.psum_tensor(f"bank{i}", [P, BANK], F32)) for i in range(BANKS)])
        step, load = S.step, S.load

        def sb(name, shape, dt=F32):
            return ctx.enter_context(nc.sbuf_tensor(name, shape, dt))

        wq = sb("wq", [P, 2, KD, F], F32R)
        wk = sb("wk", [P, 2, KD, F], F32R)
        wv = sb("wv", [P, 2, KD, F], F32R)
        wfc = sb("wfc", [P, 2, NC_F, D], F32R)
        w1 = sb("w1", [P, 2, KD, F], F32R)
        w2 = sb("w2", [P, 2, NC_F, D], F32R)
        wq1 = sb("wq1", [P, 2, KD, D], F32R)
        wkv1 = sb("wkv1", [P, KD, P + HD])
        wog = sb("wog", [P, 2, KD, 2 * D], F32R)
        wgx = sb("wgx", [P, 2, KD, D], F32R)
        NORMS = 4
        cols = sb("cols", [P, t["cols"].shape[1]])
        at = iter(np.cumsum([0] + 2 * NORMS * [KD] + [NC_F, KD, KD, 1]).tolist())
        first = [next(at) for _ in range(2 * NORMS + 5)]
        gains = [cols[:, first[i]:first[i + 1]] for i in range(NORMS)]
        shifts = [cols[:, first[NORMS + i]:first[NORMS + i + 1]] for i in range(NORMS)]
        b1, bq1, bo_col, bk1 = (cols[:, first[2 * NORMS + i]:first[2 * NORMS + i + 1]] for i in range(4))
        rows = sb("rows", [P, 5 * D + HD])
        fcb, b2, bog, rmsw, bv1 = (rows[:, i:j] for i, j in (
            (0, D), (D, 2 * D), (2 * D, 4 * D), (4 * D, 5 * D), (5 * D, 5 * D + HD)))
        ident = sb("ident", [P, P])
        center = sb("center", [P, P])
        relb = sb("relb", [P, SEQ])
        winb = sb("winb", [P, SEQ])
        block_of = sb("block_of", [P, HPC])
        head_of = sb("head_of", [P, QUAD])
        half_exp = sb("half_exp", [P, 4])
        bq = sb("bq", [P, NC_F])
        bk = sb("bk", [P, NC_F])
        bv = sb("bv", [P, NC_F])
        X = sb("X", [P, 2, GROUP, D])
        C = sb("C", [P, GROUP, D])
        NT = 2
        normed = sb("normed", [P, NT, D])
        stats = sb("stats", [P, 4, 6])
        moments = sb("moments", [P, 4, 2])
        rstd = sb("rstd", [P, 4])
        stats2 = sb("stats2", [P, GROUP, 6])
        moments2 = sb("moments2", [P, GROUP, 2])
        rstd2 = sb("rstd2", [P, GROUP])
        xT = sb("xT", [P, 2, KD, TOK], F32R)
        cT = sb("cT", [P, 2, KD, TOK], F32R)
        hT = sb("hT", [P, 2, KD, TOK], F32R)
        rawcT = sb("rawcT", [P, KD, TOK])
        qT = sb("qT", [P, QC, TOK])
        kT = sb("kT", [P, QC, TOK])
        V = sb("V", [P, GROUP, QW])
        OT = sb("OT", [P, 2, GROUP, QC, SEQ], F32R)
        NS = 4
        soft = sb("soft", [P, NS, QUAD, SEQ])
        softT = sb("softT", [P, NS, QUAD, SEQ])
        row_max = sb("row_max", [P, NS, QUAD])
        neg_max = sb("neg_max", [P, NS, QUAD])
        row_sum = sb("row_sum", [P, NS, QUAD])
        inv_sum = sb("inv_sum", [P, NS, QUAD])
        x1 = sb("x1", [P, 2, GROUP, D])
        HH = NC_F // 2
        hid = sb("hid", [P, HH, TOK])
        hidS = sb("hidS", [P, 2, HH, TOK], F32R)
        x2T = sb("x2T", [P, 2, KD, TOK], F32R)
        UW = QUAD * HD
        assert 2 * UW == P
        qS = sb("qS", [P, NU1, TOK], F32R)
        NK1 = 3
        k1T = sb("k1T", [P, NK1, TOK])
        v1 = sb("v1", [P, NK1, GROUP, HD])
        kblock = sb("kblock", [P, 2, QUAD, SEQ], F32R)
        VSTEP = UW + HD
        vpad = sb("vpad", [P, QUAD * VSTEP])
        o1T = sb("o1T", [P, 2, KD, SEQ], F32R)
        ag = sb("ag", [P, 2 * D])
        gate = sb("gate", [P, D])
        sumsq = sb("sumsq", [P, 1])
        rrms = sb("rrms", [P, 1])

        def f32(ap):
            return ap.bitcast(F32)

        def mm3(pe, out, stat, mov, first, last, **kw):
            pe.matmul(out, stat(LO), mov(HI), start=first, stop=False, **kw)
            pe.matmul(out, stat(HI), mov(LO), start=False, stop=False, **kw)
            return pe.matmul(out, stat(HI), mov(HI), start=False, stop=last, **kw)

        LOADS, SETUP = -90.0, -80.0
        S.place = -100.0
        cols_in = load("cols_in", lambda sp: sp.dma_start(cols[:], t["cols"]))

        def by_chunk(ap):
            return ap.rearrange("(k p) n -> p k n", p=P)

        consts = None
        for dst, src in ((relb[:], t["rel"]), (rows[:], t["rows"].partition_broadcast(P)),
                         (wkv1[:], by_chunk(t["wkv1"]))):
            S.place = LOADS + 1.0
            consts = load("consts", lambda sp, dst=dst, src=src: sp.dma_start(dst, src))
        S.place = SETUP
        def pool_consts(pool):
            pool.memset(half_exp[:], -0.5)
            pool.memset(ident[:], 0.0)
            pool.memset(center[:], -1.0 / SEQ)
            pool.memset(winb[:], 0.0)
            pool.memset(block_of[:], 1.0)
            return pool.memset(vpad[:], 0.0)
        filled = step("gpsimd", "filled", pool_consts)

        def pool_select(pool):
            pool.affine_select(out=ident[:], in_=ident[:], compare_op=ALU.not_equal, fill=1.0, base=0,
                               pattern=[[-1, P]], channel_multiplier=1)
            pool.affine_select(out=center[:], in_=center[:], compare_op=ALU.not_equal, fill=1.0 - 1.0 / SEQ,
                               base=0, pattern=[[-1, P]], channel_multiplier=1)
            pool.affine_select(out=winb[:], in_=winb[:], compare_op=ALU.is_ge, fill=MASKED,
                               base=WINDOW_HALF, pattern=[[1, SEQ]], channel_multiplier=-1)
            return pool.affine_select(out=block_of[:], in_=block_of[:], compare_op=ALU.is_ge, fill=0.0, base=0,
                                      pattern=[[-HD, HPC]], channel_multiplier=1)
        selected = step("gpsimd", "selected", pool_select, [filled])

        def pool_select2(pool):
            pool.affine_select(out=winb[:], in_=winb[:], compare_op=ALU.is_ge, fill=MASKED,
                               base=WINDOW_HALF, pattern=[[-1, SEQ]], channel_multiplier=1)
            return pool.affine_select(out=block_of[:], in_=block_of[:], compare_op=ALU.is_ge, fill=0.0,
                                      base=HD - 1, pattern=[[HD, HPC]], channel_multiplier=-1)
        masks = step("gpsimd", "selected", pool_select2, [selected])

        heads_made = step("gpsimd", "selected", lambda p: p.tensor_tensor(
            head_of[:], block_of[:, 0:QUAD], block_of[:, QUAD:2 * QUAD], ALU.add), [masks])

        stage = [buf.rearrange("p i n -> p (i n)") for buf in (
            soft[:, 0:2, :, :].rearrange("p s i n -> p (s i) n"),
            softT[:, 0:2, :, :].rearrange("p s i n -> p (s i) n"),
            hid[:], softT[:, 2:4, :, :].rearrange("p s i n -> p (s i) n"),
            soft[:, 2:4, :, :].rearrange("p s i n -> p (s i) n"))]
        SOFT0, SOFTT0, HID, SOFTT1, SOFT1 = range(5)
        stage_free, stage_used = [None] * 5, [None] * 5
        bias_done, split = {}, {}

        def prepare(name, slot, src, dst, gain=None, shift=None, out_bank=None, n=0):
            buf = stage[slot]
            use, S.place = S.place, LOADS
            raw = load(f"raw{slot}", lambda sp: sp.dma_start(
                buf if len(src.shape) == 2 else buf.rearrange("p (c n) -> p c n", c=src.shape[1]), src),
                [stage_free[slot], stage_used[slot]])
            used, S.place = None, use
            if gain is None:
                hi = step("scalar", "w_hi", lambda a: a.copy(dst(HI), buf), [raw])
                lo = step("vector", "w_lo", lambda v: v.tensor_tensor(
                    dst(LO), buf, f32(dst(HI)), ALU.subtract), [raw, hi])
            else:
                def bias_mm(pe):
                    for c in range(NC_F):
                        last = pe.matmul(out_bank[:, c:c + 1], buf[:, c * P:(c + 1) * P], shift,
                                         start=(n == 0 and c == 0), stop=(n == KD - 1), skip_group_check=True)
                    return last
                used = bias_done[name] = step("tensor", "bias_mm", bias_mm, [raw, cols_in, out_bank])
                hi = step("scalar", "w_hi", lambda a: a.activation(
                    dst(HI), buf, ACT.Identity, scale=gain), [raw, cols_in])
                lo = step("vector", "w_lo", lambda v: v.scalar_tensor_tensor(
                    dst(LO), buf, gain, f32(dst(HI)), ALU.mult, ALU.subtract), [raw, cols_in, hi])
            stage_free[slot], stage_used[slot] = lo, used
            split[name] = lo

        def from_norm(name, i, w, src, bias, slots):
            bank = Bank()
            for n in range(KD):
                prepare(name, slots[n], t[src][n * P:(n + 1) * P, :], lambda part, n=n: w[:, part, n, :],
                        gains[i][:, n:n + 1], shifts[i][:, n:n + 1], bank, n)
            if name == "w1":
                made = step("vector", "bias", lambda v: v.tensor_tensor(
                    bias[:], bank[:, 0:NC_F], bias[:], ALU.add), [bias_done[name], cols_in])
            else:
                made = step("vector", "bias", lambda v: v.tensor_copy(bias[:], bank[:, 0:NC_F]), [bias_done[name]])
            bank.give(made)
            bias_done[name] = made

        def plain(name, w, src, slots):
            half = NC_F // 2
            for n in range(2):
                prepare(name, slots[n], t[src][n * half * P:(n + 1) * half * P, :].rearrange("(c p) n -> p c n", p=P),
                        lambda part, n=n: w[:, part, n * half:(n + 1) * half, :].rearrange("p c n -> p (c n)"))

        from_norm("wq", 0, wq, "wq_t", bq, (SOFT0, SOFTT0))
        from_norm("wk", 1, wk, "wk_t", bk, (HID, SOFTT1))
        from_norm("wv", 2, wv, "wv_t", bv, (SOFT1, SOFT0))
        LOADS, S.place = LOADS + 2.0, 0.5
        plain("wfc", wfc, "fc_t", (SOFTT0, HID))
        S.place = 6.0
        from_norm("w1", 3, w1, "w1_t", b1, (SOFTT1, SOFT1))
        plain("w2", w2, "w2_t", (HID, SOFTT1))

        S.place = 4.0
        bcol = x1[:, 0, :, 0:P]
        bank = Bank()
        token = None
        col_read = [None, None]
        for c in range(NC_F):
            made = step("vector", "bcol_made", lambda v, c=c: v.tensor_scalar(
                bcol[:, c % 2, :], ident[:], 0.0, bv[:, c:c + 1], ALU.mult, ALU.add),
                [selected, bias_done["wv"], col_read[c % 2]])

            def fold(pe, c=c, bank=bank):
                pe.matmul(bank[:, 0:D], bcol[:, c % 2, :], f32(wfc[:, HI, c, :]), start=(c == 0), stop=False)
                return pe.matmul(bank[:, 0:D], bcol[:, c % 2, :], f32(wfc[:, LO, c, :]), start=False,
                                 stop=(c == NC_F - 1))
            col_read[c % 2] = token = step("tensor", "folded", fold, [made, split["wfc"], bank])
        fcb_ready = step("vector", "bias", lambda v, bank=bank: v.tensor_tensor(
            fcb[:], bank[:, 0:D], fcb[:], ALU.add), [token, consts])
        bank.give(fcb_ready)

        S.place = 7.0
        wo_t, wga = stage[SOFT1][:, 0:KD * D], stage[SOFT1][:, KD * D:2 * KD * D]
        got = [load(f"raw{SOFT1}", lambda sp, dst=dst, src=src: sp.dma_start(
            dst.rearrange("p (k n) -> p k n", k=KD), by_chunk(src)), [stage_free[SOFT1], stage_used[SOFT1]])
            for dst, src in ((wo_t, t["wo_t"]), (wga, t["wg"][0:D, :]))][-1:]
        for i in range(KD):
            bank = Bank()

            def wo_wg(pe, i=i, bank=bank):
                for k in range(KD):
                    last = pe.matmul(bank[:, 0:D], wo_t[:, k * D + i * P:k * D + (i + 1) * P],
                                     wga[:, k * D:(k + 1) * D], start=(k == 0), stop=(k == KD - 1))
                return last
            token = wo_wg_made = step("tensor", "wo_wg", wo_wg, got + [bank])
            hi = step("scalar", "w_hi", lambda a, i=i, bank=bank: a.copy(
                wog[:, HI, i, D:2 * D], bank[:, 0:D]), [token])
            done = step("vector", "w_lo", lambda v, i=i, bank=bank: v.tensor_tensor(
                wog[:, LO, i, D:2 * D], bank[:, 0:D], f32(wog[:, HI, i, D:2 * D]), ALU.subtract), [token, hi])
            bank.give(done)
        wo = stage[SOFTT1][:, 0:KD * D].rearrange("p (k n) -> p k n", k=KD)
        raw = load(f"raw{SOFTT1}", lambda sp: sp.dma_start(wo, by_chunk(t["wo"])), [stage_free[SOFTT1]])
        hi = step("scalar", "w_hi", lambda a: a.copy(wog[:, HI, :, 0:D], wo), [raw])
        wog_ready = stage_free[SOFTT1] = step("vector", "w_lo", lambda v: v.tensor_tensor(
            wog[:, LO, :, 0:D], wo, f32(wog[:, HI, :, 0:D]), ALU.subtract), [raw, hi])
        bank = Bank()
        for k in range(KD):
            made = step("vector", "bcol_made", lambda v, k=k: v.tensor_scalar(
                bcol[:, k % 2, :], ident[:], 0.0, bo_col[:, k:k + 1], ALU.mult, ALU.add), [col_read[k % 2], consts])
            token = step("tensor", "folded", lambda pe, k=k, bank=bank: pe.matmul(
                bank[:, 0:D], bcol[:, k % 2, :], wga[:, k * D:(k + 1) * D], start=(k == 0), stop=(k == KD - 1)),
                [made, bank] + got)
        ready = step("vector", "bias", lambda v, bank=bank: v.tensor_tensor(
            bog[:, D:2 * D], bank[:, 0:D], bog[:, D:2 * D], ALU.add), [token, consts])
        bank.give(ready)
        stage_free[SOFT1], stage_used[SOFT1] = token, wo_wg_made

        raw_q, raw_g = (stage[HID][:, i * KD * D:(i + 1) * KD * D].rearrange("p (k n) -> p k n", k=KD)
                        for i in range(2))
        for dst, src in ((raw_q, t["wq1"]), (raw_g, t["wg"][D:2 * D, :])):
            raw = load(f"raw{HID}", lambda sp, dst=dst, src=src: sp.dma_start(dst, by_chunk(src)), [stage_free[HID]])
        for w, src in ((wq1, raw_q), (wgx, raw_g)):
            hi = step("scalar", "w_hi", lambda a, w=w, src=src: a.copy(w[:, HI, :, :], src), [raw])
            stage_free[HID] = q1_gate_ready = step("vector", "w_lo", lambda v, w=w, src=src: v.tensor_tensor(
                w[:, LO, :, :], src, f32(w[:, HI, :, :]), ALU.subtract), [raw, hi])

        done = {}

        def of(stage, *index):
            return None if index[0] < 0 else done[stage, index]

        scratch_free = [None] * NT
        scratch_at = [0]
        soft_free = [[stage_free[i], stage_used[i]] for i in (SOFT0, SOFT0, SOFT1, SOFT1)]
        softT_free = [[stage_free[i], stage_used[i]] for i in (SOFTT0, SOFTT0, SOFTT1, SOFTT1)]

        def layernorm_stats(tag, sources, st, mo, rs, after):
            n = len(sources)

            def bn(v):
                for i, src in enumerate(sources):
                    last = v.bn_stats(st[:, i, :], src)
                return last
            a = step("vector", f"{tag}_stats", bn, after)

            def aggregate(v):
                for i in range(n):
                    last = v.bn_aggr(mo[:, i, :], st[:, i, :])
                return last
            a = step("vector", f"{tag}_stats", aggregate, [a])
            a = step("vector", f"{tag}_stats", lambda v: v.tensor_scalar(
                rs[:, 0:n], mo[:, 0:n, 1], EPS0, None, ALU.add), [a])
            return step("gpsimd", f"{tag}_rstd", lambda p: p.tensor_tensor(
                rs[:, 0:n], rs[:, 0:n], half_exp[:, 0:n], ALU.pow), [a, filled])

        def normalise(tag, src, mo, rs, i, after):
            slot = scratch_at[0] % NT
            scratch_at[0] += 1
            token = step("vector", f"{tag}_norm", lambda v: v.tensor_scalar(
                normed[:, slot, :], src, mo[:, i, 0:1], rs[:, i:i + 1], ALU.subtract, ALU.mult),
                list(after) + [scratch_free[slot]])
            return slot, token

        def to_feature_major(tag, pieces, after):
            bank = Bank()

            def transposes(pe):
                for b, src in enumerate(pieces):
                    for k in range(KD):
                        col = k * TOK + b * SEQ
                        last = pe.transpose(bank[:, col:col + SEQ], src[:, k * P:(k + 1) * P], ident[:])
                return last
            return bank, step("tensor", f"{tag}_turned", transposes, list(after) + [bank, selected])

        def split_out(tag, bank, dst, token, free):
            cols = slice(0, dst(HI).shape[1])
            hi = step("scalar", f"{tag}_hi", lambda a: a.copy(dst(HI), bank[:, cols]), [token] + list(free))
            lo = step("vector", f"{tag}_lo", lambda v: v.tensor_tensor(
                dst(LO), bank[:, cols], f32(dst(HI)), ALU.subtract), [token, hi] + list(free))
            bank.give(lo)
            return lo

        def fetch(g):
            s = g % 2
            done["x", (g,)] = load(f"load_x{s}", lambda sp: sp.dma_start(
                X[:, s, :, :], t["x"][g * GROUP:(g + 1) * GROUP].rearrange("b t d -> t b d")), [of("x1", g - 2)])
            done["c", (g,)] = load("load_c", lambda sp: sp.dma_start(
                C[:], t["ctx"][g * GROUP:(g + 1) * GROUP].rearrange("b t d -> t b d")),
                [of("c_norm", g - 1), of("rawc_turned", g - 1)])

        def front_stats(g):
            s = g % 2
            done["ln", (g,)] = layernorm_stats(
                "ln0", [X[:, s, b, :] for b in range(GROUP)] + [C[:, b, :] for b in range(GROUP)],
                stats, moments, rstd, [of("x", g), of("c", g), of("x_norm", g - 1), of("c_norm", g - 1)])

        def front_norm(g, which):
            name = "xc"[which]
            pieces, tokens = [], []
            for b in range(GROUP):
                src = X[:, g % 2, b, :] if which == 0 else C[:, b, :]
                slot, token = normalise(name, src, moments, rstd, which * GROUP + b, [of("ln", g)])
                pieces.append(slot)
                tokens.append(token)
            done[name + "_norm", (g,)] = tokens[-1]
            state[name, g] = pieces

        def front_turn(g, which):
            name, dst = "xc"[which], (xT, cT)[which]
            pieces = state.pop((name, g))
            bank, turned = to_feature_major(name, [normed[:, s, :] for s in pieces], [of(name + "_norm", g)])
            for s in pieces:
                scratch_free[s] = turned
            readers = [of("proj_qk", g - 1, NQ - 1)] + ([of("proj_v", g - 1, NQ - 1)] if which else [])
            lo = split_out(name, bank, lambda part: dst[:, part, :, :].rearrange("p k n -> p (k n)"), turned, readers)
            done[name + "T", (g,)] = lo

        def turn_raw(g):
            bank, turned = to_feature_major("rawc", [C[:, b, :] for b in range(GROUP)], [of("c", g)])
            done["rawc_turned", (g,)] = turned
            done["raw", (g,)] = step("scalar", "rawc_copy", lambda a: a.copy(
                rawcT[:].rearrange("p k n -> p (k n)"), bank[:]),
                                     [turned, of("proj_kv1", g - 1)])
            bank.give(done["raw", (g,)])

        def proj_kv1(g):
            bank = Bank()

            def proj(pe):
                for k in range(KD):
                    pe.matmul(bank[:, 0:TOK], wkv1[:, k, 0:P], rawcT[:, k, :], start=(k == 0), stop=(k == KD - 1))
                for b in range(GROUP):
                    for k in range(KD):
                        last = pe.matmul(bank[:, TOK + b * HD:TOK + (b + 1) * HD], rawcT[:, k, b * SEQ:(b + 1) * SEQ],
                                         wkv1[:, k, P:P + HD], start=(k == 0), stop=(k == KD - 1))
                return last
            mm = done["proj_kv1", (g,)] = step("tensor", "proj_kv1", proj, [of("raw", g), bank, consts])
            step("vector", "k1_out", lambda v: v.tensor_scalar(
                k1T[:, g % NK1, :], bank[:, 0:TOK], bk1[:, 0:1], None, ALU.add),
                [mm, of("kblock", g - NK1, GROUP - 1)])
            done["v1", (g,)] = step("vector", "k1_out", lambda v: v.tensor_tensor(
                v1[:, g % NK1, :, :], bank[:, TOK:TOK + GROUP * HD].rearrange("p (b e) -> p b e", b=GROUP),
                bv1[:].unsqueeze(1).broadcast_to([P, GROUP, HD]), ALU.add), [of("vpad", g - NK1, GROUP - 1)])
            bank.give(done["v1", (g,)])

        def proj_qk(g, Q):
            for w, src, dst, bias, name in ((wq, xT, qT, bq, "q"), (wk, cT, kT, bk, "k")):
                bank = Bank()

                def mms(pe, w=w, src=src, bank=bank):
                    for c in range(QC):
                        cols = slice((Q * QC + c) * P, (Q * QC + c + 1) * P)
                        for k in range(KD):
                            last = mm3(pe, bank[:, c * TOK:(c + 1) * TOK], lambda part: w[:, part, k, cols],
                                       lambda part: src[:, part, k, :], k == 0, k == KD - 1)
                    return last
                mm = step("tensor", "proj_qk", mms, [of("xT", g), of("cT", g), bank, split["wq"], split["wk"]])
                free = of("scores", *last_unit(*prev_quad(g, Q)))

                if name == "q":
                    def out(a, bank=bank):
                        for c in range(QC):
                            i = Q * QC + c
                            last = a.activation(qT[:, c, :], bank[:, c * TOK:(c + 1) * TOK], ACT.Identity,
                                                bias=bq[:, i:i + 1])
                        return last
                    token = step("scalar", "q_out", out, [mm, free, bias_done["wq"]])
                else:
                    def out(v, bank=bank):
                        for c in range(QC):
                            i = Q * QC + c
                            last = v.tensor_scalar(kT[:, c, :], bank[:, c * TOK:(c + 1) * TOK], bk[:, i:i + 1],
                                                   None, ALU.add)
                        return last
                    token = step("vector", "k_out", out, [mm, free, bias_done["wk"]])
                bank.give(token)
                done[name, (g, Q)] = token
            done["proj_qk", (g, Q)] = mm

        def prev_quad(g, Q):
            return (g, Q - 1) if Q else (g - 1, NQ - 1)

        def last_unit(g, Q):
            return g, 2 * Q + 1

        def proj_v(g, Q):
            bank = Bank()

            def mms(pe):
                for b in range(GROUP):
                    for k in range(KD):
                        last = mm3(pe, bank[:, b * QW:(b + 1) * QW], lambda part: cT[:, part, k, b * SEQ:(b + 1) * SEQ],
                                   lambda part: wv[:, part, k, Q * QW:(Q + 1) * QW], k == 0, k == KD - 1)
                return last
            mm = done["proj_v", (g, Q)] = step("tensor", "proj_v", mms, [of("cT", g), bank, split["wv"]])
            token = done["v", (g, Q)] = step("vector", "v_out", lambda v: v.tensor_copy(
                V[:].rearrange("p b n -> p (b n)"), bank[:]), [mm, of("pv", *prev_quad(g, Q))])
            bank.give(token)

        def biased_max(bank, bias_tile, scale, scored, slot):
            def add_max(v):
                for h in range(QUAD):
                    last = v.tensor_tensor_reduce(soft[:, slot, h, :], bank[:, h * SEQ:(h + 1) * SEQ], bias_tile[:],
                                                  1.0, LOWEST, ALU.add, ALU.max, row_max[:, slot, h:h + 1])
                return last
            m = step("vector", f"score_max{slot // 2}", add_max, [scored, *soft_free[slot], consts, masks])
            bank.give(m)
            return step("vector", f"neg_max{slot // 2}", lambda v: v.tensor_scalar(
                neg_max[:, slot, :], row_max[:, slot, :], -scale, None, ALU.mult), [m])

        def exponentials(key):
            slot, scale, m = state[key]

            def exps(a):
                for h in range(QUAD):
                    last = a.activation(soft[:, slot, h, :], soft[:, slot, h, :], ACT.Exp,
                                        bias=neg_max[:, slot, h:h + 1], scale=scale,
                                        accum_out=row_sum[:, slot, h:h + 1])
                return last
            state[key] = (slot, step("scalar", "exps" + key[0][1], exps, [m]))

        def divide(key):
            slot, e = state[key]
            r = step("vector", "sum_inv" + key[0][1], lambda v: v.reciprocal(
                inv_sum[:, slot, :], row_sum[:, slot, :]), [e])
            state[key] = (slot, step("gpsimd", "norm_" + key[0], lambda p: p.tensor_tensor(
                soft[:, slot, :, :], soft[:, slot, :, :],
                inv_sum[:, slot, :].unsqueeze(2).broadcast_to([P, QUAD, SEQ]), ALU.mult), [e, r]))

        def turn_probs(block, slot, normed_token, on_scalar):
            bank = Bank()

            def transposes(pe):
                for h in range(QUAD):
                    last = pe.transpose(bank[:, h * SEQ:(h + 1) * SEQ], soft[:, slot, h, :], ident[:])
                return last
            turned = step("tensor", f"probs{block}_turned", transposes, [normed_token, bank])
            soft_free[slot] = [turned]
            dst = softT[:, slot, :, :].rearrange("p h n -> p (h n)")
            if on_scalar:
                token = step("scalar", f"probs{block}_out_s", lambda a: a.copy(dst, bank[:]),
                             [turned, *softT_free[slot]])
            else:
                token = step("vector", f"probs{block}_out_v", lambda v: v.tensor_copy(dst, bank[:]),
                             [turned, *softT_free[slot]])
            bank.give(token)
            return token

        state = {}

        def tiles(m):
            return m // 2, m % 2 * HS, [(c, b) for c in range(QC) for b in range(GROUP)]

        def scores(g, m):
            Q, r, which = tiles(m)
            bank = Bank()

            def mms(pe):
                for h, (c, b) in enumerate(which):
                    last = pe.matmul(bank[:, h * SEQ:(h + 1) * SEQ], qT[r:r + HS, c, b * SEQ:(b + 1) * SEQ],
                                     kT[r:r + HS, c, b * SEQ:(b + 1) * SEQ], start=True, stop=True)
                return last
            mm = done["scores", (g, m)] = step("tensor", "scores", mms, [of("q", g, Q), of("k", g, Q), bank])
            slot = m % 2
            state["a0", g, m] = (slot, SCALE0, biased_max(bank, relb, SCALE0, mm, slot))

        def turn0(g, m):
            slot, token = state["a0", g, m]
            state["a0", g, m] = (slot, turn_probs(0, slot, token, m % 2 == 0))

        def pv0(g, Q):
            bank = Bank()
            units = [(slot, token, r) for slot, token, r in
                     (state.pop(("a0", g, m)) + (tiles(m)[1],) for m in (2 * Q, 2 * Q + 1))]

            def mms(pe):
                for h, (c, b) in enumerate(tiles(2 * Q)[2]):
                    col = (b * QC + c) * SEQ
                    for slot, _, r in units:
                        last = pe.matmul(bank[r:r + HS, col:col + SEQ], V[:, b, c * P + r:c * P + r + HS],
                                         softT[:, slot, h, :], start=True, stop=True)
                return last
            mm = done["pv", (g, Q)] = step("tensor", "pv", mms, [units[0][1], units[1][1], of("v", g, Q), bank])
            for slot, _, _ in units:
                softT_free[slot] = [mm]
            dst = lambda part: OT[:, part, :, :, :].rearrange("p b c n -> p (b c n)")
            state["oT"] = split_out("o", bank, dst, mm, [state.get("fc_read")])

        def fc(g, Q):
            if Q == 0:
                state["fc"] = Bank()
            bank = state["fc"]
            token = state["oT"]

            def mms(pe):
                for b in range(GROUP):
                    for c in range(QC):
                        last = mm3(pe, bank[:, b * D:(b + 1) * D], lambda part: OT[:, part, b, c, :],
                                   lambda part: wfc[:, part, Q * QC + c, :], Q == 0 and b == 0 and c == 0,
                                   Q == NQ - 1 and c == QC - 1, skip_group_check=True)
                return last
            state["fc_read"] = step("tensor", "fc", mms, [token, bank, split["wfc"]])

        def finish_attention(g):
            s = g % 2
            xs = x1[:, s, :, :]
            bank = state["fc"]
            xb = step("gpsimd", "x_plus_fcb", lambda p: p.tensor_tensor(
                X[:, s, :, :], X[:, s, :, :], fcb[:].unsqueeze(1).broadcast_to([P, GROUP, D]), ALU.add),
                [of("x", g), of("x_norm", g), fcb_ready])
            x1_done = done["x1", (g,)] = step("vector", "x1", lambda v: v.tensor_tensor(
                xs.rearrange("p b d -> p (b d)"), bank[:], X[:, s, :, :].rearrange("p b d -> p (b d)"), ALU.add),
                [state["fc_read"], xb, of("x1_read", g - 2), ready])
            bank.give(x1_done)
            rs = layernorm_stats("ln2", [xs[:, b, :] for b in range(GROUP)], stats2, moments2, rstd2, [x1_done])
            pieces, tokens = [], []
            for b in range(GROUP):
                slot, token = normalise("h", xs[:, b, :], moments2, rstd2, b, [rs])
                pieces.append(slot)
                tokens.append(token)
            done["x1b", (g,)] = step("gpsimd", "x1_plus_b2", lambda p: p.tensor_tensor(
                xs, xs, b2[:].unsqueeze(1).broadcast_to([P, GROUP, D]), ALU.add), [tokens[-1], consts])
            state["h", g] = (pieces, tokens)

        def turn_h(g):
            pieces, tokens = state.pop(("h", g))
            bank, turned = to_feature_major("h", [normed[:, s, :] for s in pieces], tokens)
            for s in pieces:
                scratch_free[s] = turned
            lo = split_out("h", bank, lambda part: hT[:, part, :, :].rearrange("p k n -> p (k n)"), turned,
                           [of("w1", g - 1, 1)])
            done["hT", (g,)] = lo

        def mlp_in(g, half, pair):
            bank = Bank()
            first = half * HH + pair * 2

            def mms(pe):
                for c in range(2):
                    for k in range(KD):
                        last = mm3(pe, bank[:, c * TOK:(c + 1) * TOK],
                                   lambda part: w1[:, part, k, (first + c) * P:(first + c + 1) * P],
                                   lambda part: hT[:, part, k, :], k == 0, k == KD - 1)
                return last
            mm = done["w1", (g, half)] = step("tensor", "w1", mms, [of("hT", g), bank, split["w1"]])

            def out(a):
                for c in range(2):
                    last = a.activation(hid[:, pair * 2 + c, :], bank[:, c * TOK:(c + 1) * TOK], ACT.Identity,
                                        bias=b1[:, first + c:first + c + 1])
                return last
            token = step("scalar", "hid_out", out, [mm, state.get("hid_read", stage_free[HID]), bias_done["w1"]])
            bank.give(token)
            state["hid"] = token

        def gelu(g, half):
            flat = hid[:].rearrange("p c n -> p (c n)")
            act = step("scalar", "gelu", lambda a: a.activation(flat, flat, ACT.Gelu), [state["hid"]])
            hi = step("vector", "hid_hi", lambda v: v.tensor_copy(
                hidS[:, HI, :, :].rearrange("p c n -> p (c n)"), flat), [act, state.get("w2_read")])
            lo = step("vector", "hid_lo", lambda v: v.tensor_tensor(
                hidS[:, LO, :, :].rearrange("p c n -> p (c n)"), flat,
                f32(hidS[:, HI, :, :]).rearrange("p c n -> p (c n)"), ALU.subtract), [hi, act])
            state["hid_read"] = lo
            state["hidS"] = lo

        def mlp_out(g, half, b):
            if half == 0 and b == 0:
                state["w2"] = Bank()
            bank = state["w2"]

            def mms(pe):
                for c in range(HH):
                    last = mm3(pe, bank[:, b * D:(b + 1) * D], lambda part: hidS[:, part, c, b * SEQ:(b + 1) * SEQ],
                               lambda part: w2[:, part, half * HH + c, :], half == 0 and b == 0 and c == 0,
                               half == 1 and c == HH - 1, skip_group_check=True)
                return last
            state["w2_read"] = step("tensor", "w2", mms, [state["hidS"], bank, split["w2"]])

        def block1_in(g):
            bank = state["w2"]
            flat = x1[:, g % 2, :, :].rearrange("p b d -> p (b d)")
            x2 = done["x2", (g,)] = step("vector", "x2", lambda v: v.tensor_tensor(flat, bank[:], flat, ALU.add),
                                         [state["w2_read"], of("x1b", g)])
            bank.give(x2)

        def turn_x2(g):
            bank, turned = to_feature_major("x2", [x1[:, g % 2, b, :] for b in range(GROUP)], [of("x2", g)])
            done["x2T", (g,)] = split_out("x2", bank, lambda part: x2T[:, part, :, :].rearrange("p k n -> p (k n)"),
                                          turned, [of("out_mm", g - 1, GROUP - 1)])

        def proj_q1(g):
            bank = Bank()

            def mms(pe):
                for c in range(KD):
                    for k in range(KD):
                        last = mm3(pe, bank[:, c * TOK:(c + 1) * TOK], lambda part: wq1[:, part, k, c * P:(c + 1) * P],
                                   lambda part: x2T[:, part, k, :], k == 0, k == KD - 1)
                return last
            mm = step("tensor", "proj_q1", mms, [of("x2T", g), bank, q1_gate_ready])

            halves = [(u, u // 2, slice(u % 2 * UW, u % 2 * UW + UW), slice((1 - u % 2) * UW, (2 - u % 2) * UW))
                      for u in range(NU1)]
            free = of("scores1", g - 1, GROUP - 1, NU1 - 1)

            def hi(a):
                for u, c, rows, _ in halves:
                    last = a.activation(qS[rows, u, :], bank[rows, c * TOK:(c + 1) * TOK], ACT.Identity,
                                        bias=bq1[rows, c:c + 1])
                return last
            high = step("scalar", "q1_out", hi, [mm, free])

            def lo(v):
                for u, c, rows, other in halves:
                    last = v.scalar_tensor_tensor(qS[other, u, :], bank[rows, c * TOK:(c + 1) * TOK],
                                                  bq1[rows, c:c + 1], f32(qS[rows, u, :]), ALU.add, ALU.subtract)
                return last
            token = done["q1", (g,)] = step("vector", "q1_lo", lo, [mm, high, free])
            bank.give(token)

        def before(g, b):
            return (g, b - 1) if b else (g - 1, GROUP - 1)

        def spread_k(g, b):
            keys = k1T[:, g % NK1, b * SEQ:(b + 1) * SEQ]
            hi = step("gpsimd", "kblock", lambda p: p.tensor_tensor(
                kblock[:, HI, :, :], keys.unsqueeze(1).broadcast_to([P, QUAD, SEQ]),
                head_of[:].unsqueeze(2).broadcast_to([P, QUAD, SEQ]), ALU.mult),
                [of("v1", g), of("scores1", *before(g, b), NU1 - 1), heads_made])

            def low(v):
                for h in range(QUAD):
                    last = v.scalar_tensor_tensor(kblock[:, LO, h, :], keys, head_of[:, h:h + 1],
                                                  f32(kblock[:, HI, h, :]), ALU.mult, ALU.subtract)
                return last
            done["kblock", (g, b)] = step("vector", "kblock_lo", low, [hi])

        def spread_v(g, b):
            done["vpad", (g, b)] = step("gpsimd", "vpad", lambda p: p.tensor_copy(
                vpad[:].rearrange("p (j n) -> p j n", n=VSTEP)[:, :, 0:HD],
                v1[:, g % NK1, b, :].unsqueeze(1).broadcast_to([P, QUAD, HD])),
                [of("v1", g), of("pv1", *before(g, b), KD - 1), filled])

        def scores1(g, b, u):
            bank = Bank()
            rows, cols = slice(u % 2 * UW, u % 2 * UW + UW), slice(b * SEQ, (b + 1) * SEQ)

            def mms(pe):
                pe.matmul(bank[:], qS[rows, u, cols], kblock[rows, LO, :, :], start=True, stop=False)
                return pe.matmul(bank[:], qS[:, u, cols], kblock[:, HI, :, :], start=False, stop=True)
            mm = done["scores1", (g, b, u)] = step("tensor", "scores1", mms, [of("q1", g), of("kblock", g, b), bank])
            slot = (2 + u) % NS if g == NG - 1 else 2 + u % 2
            state["a1", g, b, u] = (slot, SCALE1, biased_max(bank, winb, SCALE1, mm, slot))

        def turn1(g, b, u):
            slot, token = state["a1", g, b, u]
            state["a1", g, b, u] = (slot, turn_probs(1, slot, token, u % 2 == 1))

        def pv1(g, b, c):
            if c == 0:
                state["o1"] = Bank()
            bank = state["o1"]
            units = [(slot, token, i * UW) for i, (slot, token) in
                     enumerate(state.pop(("a1", g, b, 2 * c + i)) for i in range(2))]

            def mms(pe):
                for h in range(QUAD):
                    for slot, _, r in units:
                        last = pe.matmul(bank[r:r + UW, c * SEQ:(c + 1) * SEQ], vpad[:, h * UW:(h + 1) * UW],
                                         softT[:, slot, h, :], start=(h == 0), stop=(h == QUAD - 1))
                return last
            mm = done["pv1", (g, b, c)] = step("tensor", "pv1", mms,
                                               [units[0][1], units[1][1], of("vpad", g, b), bank])
            for slot, _, _ in units:
                softT_free[slot] = [mm]
            if c == KD - 1:
                pg, pb = before(g, b)
                done["o1", (g, b)] = split_out(
                    "o1", bank, lambda part: o1T[:, part, :, :].rearrange("p c n -> p (c n)"), mm, [of("out_mm", pg, pb)])

        def out_mm(g, b):
            bank = Bank()

            def mms(pe):
                for k in range(KD):
                    last = mm3(pe, bank[:], lambda part: o1T[:, part, k, :], lambda part: wog[:, part, k, :],
                               k == 0, k == KD - 1, skip_group_check=True)
                    if k == 0:
                        for i in range(KD):
                            mm3(pe, bank[:, D:2 * D], lambda part: x2T[:, part, i, b * SEQ:(b + 1) * SEQ],
                                lambda part: wgx[:, part, i, :], False, False, skip_group_check=True)
                return last
            mm = done["out_mm", (g, b)] = step("tensor", "out_mm", mms, [
                of("o1", g, b), of("x2T", g), bank, wog_ready, q1_gate_ready])
            att, z = ag[:, 0:D], ag[:, D:2 * D]
            read = of("mix_read", *before(g, b))
            a0 = step("vector", "ag", lambda v: v.tensor_tensor(ag[:], bank[:], bog[:], ALU.add), [mm, read, ready])
            bank.give(a0)
            th = step("scalar", "tanh", lambda a: a.activation(gate[:], z, ACT.Tanh, scale=0.5),
                      [a0, of("stored", g * GROUP + b - 1)])
            df = step("gpsimd", "mix", lambda p: p.tensor_tensor(att, att, x1[:, g % 2, b, :], ALU.subtract), [a0])
            g1 = step("vector", "gate", lambda v: v.tensor_scalar(gate[:], gate[:], 0.5, 0.5, ALU.mult, ALU.add), [th])
            g2 = step("gpsimd", "mix", lambda p: p.tensor_tensor(gate[:], gate[:], z, ALU.mult), [g1])
            m1 = step("gpsimd", "mix", lambda p: p.tensor_tensor(att, att, gate[:], ALU.mult), [g2, df])
            m2 = step("gpsimd", "mix", lambda p: p.tensor_tensor(att, att, x1[:, g % 2, b, :], ALU.add), [m1])
            if b == GROUP - 1:
                done["x1_read", (g,)] = m2
            sq = step("scalar", "square", lambda a: a.activation(gate[:], att, ACT.Square,
                                                                 accum_out=sumsq[:, 0:1]), [m2])
            ms = step("vector", "gate", lambda v: v.tensor_scalar(
                rrms[:], sumsq[:], 1.0 / D, EPS1, ALU.mult, ALU.add), [sq, read])
            rr = step("gpsimd", "rrms", lambda p: p.tensor_tensor(rrms[:], rrms[:], half_exp[:, 0:1], ALU.pow), [ms])
            xh = step("vector", "x_hat", lambda v: v.scalar_tensor_tensor(
                att, att, rrms[:, 0:1], rmsw[:], ALU.mult, ALU.mult), [rr, sq, m2])
            state["xhat", g, b] = xh

        def center_out(g, b):
            xh = state.pop(("xhat", g, b))
            bank = Bank()
            mm = done["mix_read", (g, b)] = step("tensor", "center", lambda pe: pe.matmul(
                bank[:, 0:D], center[:], ag[:, 0:D], start=True, stop=True), [xh, bank, selected])
            n = g * GROUP + b
            y = step("scalar", "y_out", lambda a: a.copy(gate[:], bank[:, 0:D]), [mm])
            bank.give(y)
            done["stored", (n,)] = load("store", lambda sp: sp.dma_start(t["out"][n], gate[:]), [y])

        UNITS = NQ * 2
        MLP_SPAN, BLOCK1_SPAN = 2.01, 8.6
        work = []

        def spread(start, span, pieces):
            work.extend((start + i * span / len(pieces), piece) for i, piece in enumerate(pieces))

        def ahead(steps, piece):
            def early():
                S.place -= steps
                piece()
                S.place += steps
            return early

        def attention_pieces(n):
            g, m = n // UNITS, n % UNITS
            unit = lambda n: (n // UNITS, n % UNITS)
            running = n < NG * UNITS
            pieces = []
            if running:
                pieces.append(lambda: scores(g, m))
            k = n - 3
            if k >= 1 and k % 2 == 1 and k < NG * UNITS:
                kg, kq = k // UNITS, (k % UNITS) // 2
                pieces.append(lambda: fc(kg, kq))
                if kq == NQ - 1:
                    pieces.append(lambda: finish_attention(kg))
            if running and m == 1:
                pieces.append(lambda: turn_raw(g))
            if running and m == 2:
                pieces.append(lambda: proj_kv1(g))
            if running:
                pieces.append(lambda: exponentials(("a0", g, m)))
            if g + 1 < NG:
                if m == 3:
                    pieces.append(lambda: fetch(g + 1))
                if m == 4:
                    pieces.append(lambda: front_stats(g + 1))
                if m == 5:
                    pieces.append(lambda: front_norm(g + 1, 0))
                if m == UNITS - 2:
                    pieces.append(ahead(0.65, lambda: (front_turn(g + 1, 0), front_norm(g + 1, 1))))
            gq, q = (g, m // 2 + 1) if m // 2 + 1 < NQ else (g + 1, 0)
            if k >= 0 and k % 2 == 0 and k < NG * UNITS:
                pieces.append(ahead(0.17, lambda: pv0(k // UNITS, (k % UNITS) // 2)))
                nq = k // 2 + 1
                if nq < NG * NQ:
                    pieces.append(ahead(0.25, lambda: proj_v(nq // NQ, nq % NQ)))
            if g + 1 < NG and m == UNITS - 1:
                pieces.append(ahead(0.65, lambda: front_turn(g + 1, 1)))
            if gq < NG and m % 2 == 1:
                pieces.append(lambda: proj_qk(gq, q))
            if running:
                pieces.append(lambda: divide(("a0", g, m)))
            if 1 <= n and n - 1 < NG * UNITS:
                pieces.append(lambda: turn0(*unit(n - 1)))
            return pieces

        def mlp_pieces(g):
            into = lambda half, pair: lambda: mlp_in(g, half, pair)
            act = lambda half: lambda: gelu(g, half)
            out = lambda half, b: lambda: mlp_out(g, half, b)
            return [lambda: turn_h(g), into(0, 0), into(0, 1), act(0), into(1, 0), out(0, 0), out(0, 1),
                    into(1, 1), act(1), out(1, 0), out(1, 1), lambda: block1_in(g)]

        def block1_pieces(g):
            pieces = [lambda: (spread_k(g, 0), spread_v(g, 0)), lambda: turn_x2(g), lambda: proj_q1(g)]
            units = [(b, u) for b in range(GROUP) for u in range(NU1)]
            for n in range(len(units) + 4):
                if n < len(units):
                    b, u = units[n]
                    pieces.append(lambda b=b, u=u: (scores1(g, b, u), exponentials(("a1", g, b, u)),
                                                    divide(("a1", g, b, u))))
                    if u == NU1 - 1 and b + 1 < GROUP:
                        pieces.append(lambda b=b: spread_k(g, b + 1))
                if n % 2 == 1 and 0 <= n - 3 < len(units):
                    b, u = units[n - 3]
                    pieces.append(lambda b=b, u=u: pv1(g, b, u // 2))
                    if u // 2 == KD - 1 and b + 1 < GROUP:
                        pieces.append(lambda b=b: spread_v(g, b + 1))
                if 1 <= n and n - 1 < len(units):
                    b, u = units[n - 1]
                    pieces.append(lambda b=b, u=u: turn1(g, b, u))
                if 4 <= n and units[n - 4][1] == NU1 - 1:
                    b = units[n - 4][0]
                    pieces.append(lambda b=b: (out_mm(g, b), center_out(g, b)))
            return pieces

        work.append((-95.0, lambda: fetch(0)))
        spread(SETUP, 1.0, [lambda: front_stats(0), lambda: front_norm(0, 0),
                           lambda: front_turn(0, 0), lambda: front_norm(0, 1), lambda: front_turn(0, 1),
                           lambda: proj_qk(0, 0), lambda: proj_v(0, 0)])
        for n in range(NG * UNITS + 4):
            spread(n, 1.0, attention_pieces(n))
        for g in range(NG):
            start = (g + 1) * UNITS + 3.35
            spread(start, MLP_SPAN, mlp_pieces(g))
            spread(start + MLP_SPAN, BLOCK1_SPAN, block1_pieces(g))
        for S.place, piece in sorted(work, key=lambda w: w[0]):
            piece()
        S.order()
        name, value = done["stored", (NBATCH - 1,)]
        fin = [(S.sem[name], value)]

        block = ctx.enter_context(nc.Block())

        @block.sync
        def _(eng):
            S.replay("sync", eng)
            for sem, value in fin:
                eng.wait_ge(sem, value)

        @block.tensor
        def _(eng):
            S.replay("tensor", eng)

        @block.vector
        def _(eng):
            S.replay("vector", eng)

        @block.scalar
        def _(eng):
            S.replay("scalar", eng)

        @block.gpsimd
        def _(eng):
            S.replay("gpsimd", eng)


def kernel(x, ctx_1024, **w):
    import concourse.bacc as bacc
    from concourse.bass_utils import run_bass_kernel_spmd

    D = x.shape[2]
    T = x.shape[1]
    a = {k.replace("L0_xattn_", "0").replace("L1_xattn_", "1"): v for k, v in w.items()}
    rel = a["0rel_bias"]
    ntok = (rel.shape[0] + 1) // 2

    def columns(v):
        return v.reshape(-1, P).T

    norms = ("0ln_q", "0ln_k", "0ln_v", "0ln2")
    heads_in_chunk = P // a["1Wk"].shape[1]
    arrays = {
        "x": x, "ctx": ctx_1024,
        "wq_t": a["0Wq"].reshape(-1, D).T, "wk_t": a["0Wk"].reshape(-1, D).T, "wv_t": a["0Wv"].reshape(-1, D).T,
        "fc_t": a["0fc_w"].T, "w1_t": a["0W1"].T, "w2_t": a["0W2"].T,
        "rel": np.stack([rel[r + ntok - T:r + ntok][::-1] for r in range(T)]),
        "cols": np.concatenate([columns(a[n + "_g"]) for n in norms] + [columns(a[n + "_b"]) for n in norms] + [
            columns(a["0b1"]), columns(a["1bq"]), columns(a["1bo"]),
            columns(np.tile(a["1bk"], heads_in_chunk))], axis=1),
        "rows": np.concatenate([a["0fc_b"], a["0b2"], a["1bo"], a["1bg"], a["1rms_w"], a["1bv"]]),
        "wkv1": np.concatenate([np.tile(a["1Wk"], (1, heads_in_chunk)), a["1Wv"]], axis=1),
        "wq1": a["1Wq"], "wo": a["1Wo"], "wo_t": a["1Wo"].T, "wg": a["1Wg"],
    }
    nc = bacc.Bacc("TRN2", target_bir_lowering=False, num_devices=1)
    ins, tensors = {}, {}
    for name, v in arrays.items():
        v = np.ascontiguousarray(v)
        ins[f"in_{name}"] = v
        tensors[name] = nc.dram_tensor(f"in_{name}", v.shape, mybir.dt.from_np(v.dtype), kind="ExternalInput").ap()
    tensors["out"] = nc.dram_tensor("out_0", x.shape, F32, kind="ExternalOutput").ap()
    two_block_xattn(nc, tensors)
    r = run_bass_kernel_spmd(nc, [ins], core_ids=[0])
    return r.results[0]["out_0"]
```
